# Optimizing a Trainium2 kernel written in Bass

```python
import numpy as np
import jax
import jax.numpy as jnp

def _softmax(x, axis=-1):
    return jax.nn.softmax(x, axis=axis)

def _gelu(x):
    return jax.nn.gelu(x, approximate=True)

def _silu(x):
    return jax.nn.silu(x)

def _sigmoid(x):
    return jax.nn.sigmoid(x)

def _layernorm(x, axis=-1, eps=1e-05):
    m = jnp.mean(x, axis=axis, keepdims=True)
    v = jnp.var(x, axis=axis, keepdims=True)
    return (x - m) / jnp.sqrt(v + eps)

def _scatter_add(tgt, idx, src, axis=0):
    return tgt.at[idx].add(src)

def _segment_sum(src, seg, n):
    return jax.ops.segment_sum(src, seg, n)
kernel_name = 'mk_cond_seq_d2_seqx_r4_63f1ce'

def setup_inputs(seed: int=0):
    np.random.seed(seed)
    _w = jnp.asarray

    def _rec_inputs():
        import jax
        import jax.numpy as jnp
        _rk = jax.random.key(seed)
        x = 7.22e-05 + 1 * jax.random.normal(jax.random.fold_in(_rk, 1), (64, 64, 256), jnp.float32)
        _lenS = 64 - jax.random.randint(jax.random.fold_in(_rk, 7), (64,), 0, max(1, 64 // 4) + 1, jnp.int32)
        _lenS2 = 64 - jax.random.randint(jax.random.fold_in(_rk, 8), (64,), 0, max(1, 64 // 4) + 1, jnp.int32)
        cond_256 = -0.0209273 + 1.04763 * jax.random.normal(jax.random.fold_in(_rk, 11), (64, 64), jnp.float32)
        return (x, cond_256)
    x, cond_256 = _rec_inputs()

    def _L0_cond_setup():
        import jax, jax.numpy as jnp
        import numpy as np
        from math import sqrt
        D_MODEL = 256
        N_HEADS = 16
        D_T = 64
        D_HID = 4 * D_MODEL
        EPS = 1e-06

        def _rmsnorm(x):
            return x * jax.lax.rsqrt(jnp.mean(x * x, axis=-1, keepdims=True) + EPS)

        def _ada_rmsnorm(x, t, gamma_w, beta_w):
            gamma = (t @ gamma_w.T)[:, None, :]
            beta = (t @ beta_w.T)[:, None, :]
            return gamma * _rmsnorm(x) + beta

        def _attention(x, W_q, W_k, W_v, W_o):
            b, l, dm = x.shape
            d_head = dm // N_HEADS
            scale = sqrt(N_HEADS / dm)

            def split(y):
                return y.reshape(b, l, N_HEADS, d_head).transpose(0, 2, 1, 3)
            q = split(x @ W_q.T)
            k = split(x @ W_k.T)
            v = split(x @ W_v.T)
            attn = jax.nn.softmax(scale * jnp.einsum('bnqd,bnkd->bnqk', q, k), axis=-1)
            o = jnp.einsum('bnqk,bnkd->bnqd', attn, v)
            o = o.transpose(0, 2, 1, 3).reshape(b, l, dm)
            return o @ W_o.T

        def _swiglu(x, gate_w, hidden_w, out_w, out_b):
            return jax.nn.silu(x @ gate_w.T) * (x @ hidden_w.T) @ out_w.T + out_b
        key = jax.random.key(seed)
        ks = jax.random.split(key, 16)
        s = 0.02
        inp = {'x': jax.random.normal(ks[0], (4, 512, D_MODEL), dtype=jnp.float32), 't': jax.random.normal(ks[1], (4, D_T), dtype=jnp.float32), 'attn_gamma_w': jax.random.normal(ks[2], (D_MODEL, D_T), dtype=jnp.float32) * s, 'attn_beta_w': jax.random.normal(ks[3], (D_MODEL, D_T), dtype=jnp.float32) * s, 'W_q': jax.random.normal(ks[4], (D_MODEL, D_MODEL), dtype=jnp.float32) * s, 'W_k': jax.random.normal(ks[5], (D_MODEL, D_MODEL), dtype=jnp.float32) * s, 'W_v': jax.random.normal(ks[6], (D_MODEL, D_MODEL), dtype=jnp.float32) * s, 'W_o': jax.random.normal(ks[7], (D_MODEL, D_MODEL), dtype=jnp.float32) * s, 'attn_alpha_w': jax.random.normal(ks[8], (D_MODEL, D_T), dtype=jnp.float32) * s, 'ffn_gamma_w': jax.random.normal(ks[9], (D_MODEL, D_T), dtype=jnp.float32) * s, 'ffn_beta_w': jax.random.normal(ks[10], (D_MODEL, D_T), dtype=jnp.float32) * s, 'gate_w': jax.random.normal(ks[11], (D_HID, D_MODEL), dtype=jnp.float32) * s, 'hidden_w': jax.random.normal(ks[12], (D_HID, D_MODEL), dtype=jnp.float32) * s, 'out_w': jax.random.normal(ks[13], (D_MODEL, D_HID), dtype=jnp.float32) * s, 'out_b': jnp.zeros((D_MODEL,), dtype=jnp.float32), 'ffn_alpha_w': jax.random.normal(ks[14], (D_MODEL, D_T), dtype=jnp.float32) * s}
        return inp
    _L0_cond_all = _L0_cond_setup()
    _L0_cond_in = {k: v for k, v in _L0_cond_all.items() if k in ('attn_gamma_w', 'attn_beta_w', 'W_q', 'W_k', 'W_v', 'W_o', 'attn_alpha_w', 'ffn_gamma_w', 'ffn_beta_w', 'gate_w', 'hidden_w', 'out_w', 'out_b', 'ffn_alpha_w')}
    del _L0_cond_all

    def _L1_cond_setup():
        import jax, jax.numpy as jnp
        import numpy as np
        EPS = 1e-05
        key = jax.random.key(seed)
        k1, k2, k3, k4 = jax.random.split(key, 4)
        b, t, d, num_con = (8, 1024, 256, 64)
        return {'input': jax.random.normal(k1, (b, t, d), dtype=jnp.float32), 'convInfo': jax.random.normal(k2, (b, num_con), dtype=jnp.float32), 'weight': jnp.ones((d,), dtype=jnp.float32), 'bias': jnp.zeros((d,), dtype=jnp.float32), 'lin_w': jax.random.normal(k3, (d, num_con), dtype=jnp.float32) * (1.0 / np.sqrt(num_con)), 'lin_b': jax.random.normal(k4, (d,), dtype=jnp.float32) * 0.01}
    _L1_cond_all = _L1_cond_setup()
    _L1_cond_in = {k: v for k, v in _L1_cond_all.items() if k in ('weight', 'bias', 'lin_w', 'lin_b')}
    del _L1_cond_all
    return {'x': x, 'cond_256': cond_256, 'L0_cond_attn_gamma_w': _L0_cond_in['attn_gamma_w'], 'L0_cond_attn_beta_w': _L0_cond_in['attn_beta_w'], 'L0_cond_W_q': _L0_cond_in['W_q'], 'L0_cond_W_k': _L0_cond_in['W_k'], 'L0_cond_W_v': _L0_cond_in['W_v'], 'L0_cond_W_o': _L0_cond_in['W_o'], 'L0_cond_attn_alpha_w': _L0_cond_in['attn_alpha_w'], 'L0_cond_ffn_gamma_w': _L0_cond_in['ffn_gamma_w'], 'L0_cond_ffn_beta_w': _L0_cond_in['ffn_beta_w'], 'L0_cond_gate_w': _L0_cond_in['gate_w'], 'L0_cond_hidden_w': _L0_cond_in['hidden_w'], 'L0_cond_out_w': _L0_cond_in['out_w'], 'L0_cond_out_b': _L0_cond_in['out_b'], 'L0_cond_ffn_alpha_w': _L0_cond_in['ffn_alpha_w'], 'L1_cond_weight': _L1_cond_in['weight'], 'L1_cond_bias': _L1_cond_in['bias'], 'L1_cond_lin_w': _L1_cond_in['lin_w'], 'L1_cond_lin_b': _L1_cond_in['lin_b']}

def reference(x, cond_256, L0_cond_attn_gamma_w, L0_cond_attn_beta_w, L0_cond_W_q, L0_cond_W_k, L0_cond_W_v, L0_cond_W_o, L0_cond_attn_alpha_w, L0_cond_ffn_gamma_w, L0_cond_ffn_beta_w, L0_cond_gate_w, L0_cond_hidden_w, L0_cond_out_w, L0_cond_out_b, L0_cond_ffn_alpha_w, L1_cond_weight, L1_cond_bias, L1_cond_lin_w, L1_cond_lin_b):
    import jax
    import jax.numpy as jnp

    def _L0_cond_ref(x, t, attn_gamma_w, attn_beta_w, W_q, W_k, W_v, W_o, attn_alpha_w, ffn_gamma_w, ffn_beta_w, gate_w, hidden_w, out_w, out_b, ffn_alpha_w):
        import jax, jax.numpy as jnp
        import numpy as np
        from math import sqrt
        D_MODEL = 256
        N_HEADS = 16
        D_T = 64
        D_HID = 4 * D_MODEL
        EPS = 1e-06

        def _rmsnorm(x):
            return x * jax.lax.rsqrt(jnp.mean(x * x, axis=-1, keepdims=True) + EPS)

        def _ada_rmsnorm(x, t, gamma_w, beta_w):
            gamma = (t @ gamma_w.T)[:, None, :]
            beta = (t @ beta_w.T)[:, None, :]
            return gamma * _rmsnorm(x) + beta

        def _attention(x, W_q, W_k, W_v, W_o):
            b, l, dm = x.shape
            d_head = dm // N_HEADS
            scale = sqrt(N_HEADS / dm)

            def split(y):
                return y.reshape(b, l, N_HEADS, d_head).transpose(0, 2, 1, 3)
            q = split(x @ W_q.T)
            k = split(x @ W_k.T)
            v = split(x @ W_v.T)
            attn = jax.nn.softmax(scale * jnp.einsum('bnqd,bnkd->bnqk', q, k), axis=-1)
            o = jnp.einsum('bnqk,bnkd->bnqd', attn, v)
            o = o.transpose(0, 2, 1, 3).reshape(b, l, dm)
            return o @ W_o.T

        def _swiglu(x, gate_w, hidden_w, out_w, out_b):
            return jax.nn.silu(x @ gate_w.T) * (x @ hidden_w.T) @ out_w.T + out_b
        a_alpha = (t @ attn_alpha_w.T)[:, None, :]
        x = x + a_alpha * _attention(_ada_rmsnorm(x, t, attn_gamma_w, attn_beta_w), W_q, W_k, W_v, W_o)
        f_alpha = (t @ ffn_alpha_w.T)[:, None, :]
        return x + f_alpha * _swiglu(_ada_rmsnorm(x, t, ffn_gamma_w, ffn_beta_w), gate_w, hidden_w, out_w, out_b)

    def _L1_cond_ref(input, convInfo, weight, bias, lin_w, lin_b):
        import jax, jax.numpy as jnp
        import numpy as np
        EPS = 1e-05
        mean = jnp.mean(input, axis=-1, keepdims=True)
        var = jnp.mean(jnp.square(input - mean), axis=-1, keepdims=True)
        out = (input - mean) * jax.lax.rsqrt(var + EPS) * weight + bias
        tar_bias = jnp.tanh(convInfo @ lin_w.T + lin_b)[:, None, :]
        out = out + tar_bias
        return out * weight + bias
    x = _L0_cond_ref(x, cond_256, L0_cond_attn_gamma_w, L0_cond_attn_beta_w, L0_cond_W_q, L0_cond_W_k, L0_cond_W_v, L0_cond_W_o, L0_cond_attn_alpha_w, L0_cond_ffn_gamma_w, L0_cond_ffn_beta_w, L0_cond_gate_w, L0_cond_hidden_w, L0_cond_out_w, L0_cond_out_b, L0_cond_ffn_alpha_w)
    x = _L1_cond_ref(x, cond_256, L1_cond_weight, L1_cond_bias, L1_cond_lin_w, L1_cond_lin_b)
    return x

_drawn_inputs = setup_inputs


def setup_inputs(seed=0):
    import zlib

    import numpy as np

    out = dict(_drawn_inputs(seed))
    spreads = {'L0_cond_out_b': (0.0, 0.573), 'L1_cond_weight': (1.0, 0.2), 'L1_cond_bias': (0.0, 0.1)}
    factors = {'L0_cond_attn_gamma_w': 8.0,
     'L0_cond_attn_beta_w': 8.0,
     'L0_cond_W_q': 8.0,
     'L0_cond_W_k': 8.0,
     'L0_cond_W_v': 8.0,
     'L0_cond_W_o': 8.0,
     'L0_cond_attn_alpha_w': 8.0,
     'L0_cond_ffn_gamma_w': 8.0,
     'L0_cond_ffn_beta_w': 8.0,
     'L0_cond_gate_w': 8.0,
     'L0_cond_hidden_w': 8.0,
     'L0_cond_out_w': 8.0,
     'L0_cond_ffn_alpha_w': 3.972,
     'L1_cond_lin_b': 8.0}
    for name, (base, spread) in spreads.items():
        noise = np.random.default_rng([zlib.crc32(name.encode()), seed]).standard_normal(out[name].shape)
        drawn = base * np.exp(spread * noise) if base else spread * noise
        out[name] = jnp.asarray(drawn.astype(out[name].dtype))
    for name, factor in factors.items():
        out[name] = (out[name] * factor).astype(out[name].dtype)
    return out
```

```python
from contextlib import ExitStack

import numpy as np

import concourse.bass as bass
from concourse import mybir

F32, F32R, BF16, I32 = mybir.dt.float32, mybir.dt.float32r, mybir.dt.bfloat16, mybir.dt.int32
ALU, ACT, AX = mybir.AluOpType, mybir.ActivationFunctionType, mybir.AxisListType

P = 128
B, L, D = 64, 64, 256
HEADS, DH = 16, 16
DT = 64
HID = 4 * D
KD = D // P
SEQ = 8
TOK = SEQ * L
GROUPS = B // SEQ
TT = TOK // P
G = 2
J = 4
CH = HID // P
SCALE = (HEADS / D) ** 0.5
EPS_RMS, EPS_LN = 1e-6, 1e-5
NEWTON = 3
LD_CONST = 16 * 9
SETUP_TANH, SETUP_SHIFT = 1, 5
ZEROED = 3
RSQRT_MAGIC = float(0x5F3759DF)
TABLES = ("attn_gamma", "attn_beta", "attn_alpha", "ffn_gamma", "ffn_beta", "ffn_alpha")
GA, BA, AA, GF, BF, AF = range(6)

C_ID, C_PAR, C_NEG, C_BLK, C_ONE, C_ROW = 0, 128, 130, 134, 166, 198
C_END = C_ROW + TT * P


def shape_constants():
    c = np.zeros((P, C_END), np.float32)
    p = np.arange(P)
    c[p, C_ID + p] = 1
    c[p, C_PAR + (p // DH) % 2] = 1
    c[p, C_NEG + p % J] = -1
    for e in range(2):
        c[64 * e:64 * e + 64, C_BLK + DH * e:C_BLK + DH * e + DH] = 1
    c[:, C_ONE:C_ONE + 32] = 1
    for t in range(TT):
        c[32 * t, C_ROW + P * t:C_ROW + P * t + P] = 1
    sel = np.zeros((P, G * SEQ, 2, 64), np.float32)
    for r in range(P):
        sel[r, (r % 64) // J, r // 64, :] = 1
    return c, sel.reshape(P, G * SEQ * P)


def build(nc, x, xT, condT, tabT, linT, linb, lnw, lnb, wqkT, wvT, woT, ghT, outT, outb_dram,
          consts, sel_dram, out):
    with ExitStack() as ctx:
        def sb(name, shape, dt=F32):
            return ctx.enter_context(nc.sbuf_tensor(name, shape, dt))

        def sem(name):
            return ctx.enter_context(nc.semaphore(name))

        cst = sb("cst", [P, C_END])
        sel = sb("sel", [P, G * SEQ, P], BF16)
        identb = sb("identb", [P, 64], BF16)
        wqk = sb("wqk", [P, 2, KD, 2 * D], F32R)
        wv = sb("wv", [P, KD, D])
        wo = sb("wo", [P, 2, KD, D], F32R)
        gh = sb("gh", [P, 2, KD, 2 * HID], F32R)
        wout = sb("wout", [P, 2, CH, D], F32R)
        outb = sb("outb", [P, KD])
        tabs = sb("tabs", [P, len(TABLES), KD, B])
        w2 = sb("w2", [P, D])
        xtok = sb("xtok", [P, TT, D])
        xres = sb("xres", [P, KD, TOK])
        xn = sb("xn", [P, KD, TOK])
        xs = sb("xs", [P, 2, KD, TOK], F32R)
        qT = sb("qT", [P, G, TOK])
        kTb = sb("kTb", [P, G, TOK], BF16)
        qpar = sb("qpar", [P, G, SEQ, 2, L], BF16)
        kpar = sb("kpar", [P, G, SEQ, 2, L])
        qpair = sb("qpair", [P, G, J, TOK])
        kpair = sb("kpair", [P, G, J, TOK], BF16)
        vblk = sb("vblk", [P, SEQ, G * J, 2, DH])
        smax = sb("smax", [P, G * SEQ * J], BF16)
        negmax = sb("negmax", [P, J, L], BF16)
        pt = sb("pt", [P, SEQ, J, L])
        work_b = sb("work_b", [P, KD, TOK])
        work_c = sb("work_c", [P, 2, TOK])
        work_d = sb("work_d", [P, KD, TOK])
        os_ = sb("os", [P, 2, G, TOK], F32R)
        x2 = sb("x2", [P, KD, TOK])
        x2s = sb("x2s", [P, 2, KD, TOK], F32R)
        act_t = sb("act_t", [P, 2, TOK])
        hs = sb("hs", [P, 2, 2, TOK], F32R)
        final = sb("final", [P, TT, D])
        shift = sb("shift", [P, TT, D])
        stat = sb("stat", [P, 2, TT, 6])
        mv = sb("mv", [P, 2, TT, 2])
        nt1 = sb("nt1", [P, 3, TT])
        nt3 = sb("nt3", [P, 4, TT])
        nt2 = sb("nt2", [P, 3, P])
        banks = ctx.enter_context(nc.psum_tensor("banks", [P, 8, 512], F32))
        shift_dram = nc.dram_tensor("shift_dram", [B, D], F32, kind="Internal").ap()

        ident = cst[:, C_ID:C_ID + P]
        setup_area = pt[0:DT].rearrange("p b j q -> p (b j q)")
        n_tab = len(TABLES) * D
        tabw = setup_area[:, 0:n_tab].rearrange("p (t n) -> p t n", n=D)
        linw = setup_area[:, n_tab:n_tab + D]
        cond = setup_area[:, n_tab + D:n_tab + D + B]
        lnw_b, lnb_b, linb_b = final[:, 0, :], final[:, 1, :], final[:, 2, :]
        cvec = final[:, 3, :]
        v_psum = banks[:, 6:8, :].rearrange("p k (b j d) -> p (k b) j d", b=4, d=DH)
        max_t = banks[:, 6, :].bitcast(BF16)[:, 0:L]


        ld_const, ld_x, ld_res, ld_shift = map(sem, ("ld_const", "ld_x", "ld_res", "ld_shift"))
        ld_stage = (sem("ld_stage0"), sem("ld_stage1"))
        kpair_moved, qpair_moved, out_stored, shift_stored = map(
            sem, ("kpair_moved", "qpair_moved", "out_stored", "shift_stored"))
        zeroed = sem("zeroed")
        tables_mm, tables_ready, identb_ready, setup_dve, setup_act = map(
            sem, ("tables_mm", "tables_ready", "identb_ready", "setup_dve", "setup_act"))
        stage_hi, stage_lo = sem("stage_hi"), sem("stage_lo")
        k_mm, q_mm, v_mm, s_mm, mt_mm, st_mm, den_mm, o_mm, xt_mm, op_mm, ss_mm, rb_mm, gate_mm, hidden_mm, out_mm, ft_mm = map(
            sem, ("k_mm", "q_mm", "v_mm", "s_mm", "mt_mm", "st_mm", "den_mm", "o_mm", "xt_mm", "op_mm", "ss_mm",
                  "rb_mm", "gate_mm", "hidden_mm", "out_mm", "ft_mm"))
        k_ready, q_ready, v_ready, max_ready, negmax_ready, p_ready = map(
            sem, ("k_ready", "q_ready", "v_ready", "max_ready", "negmax_ready", "p_ready"))
        norm1_steps, xs_scaled, xn_gamma, xn_beta, xs_hi, xs_lo = map(
            sem, ("norm1_steps", "xs_scaled", "xn_gamma", "xn_beta", "xs_hi", "xs_lo"))
        o_steps, o_hi, o_lo, x2_steps, sq_ready, x2_gamma = map(
            sem, ("o_steps", "o_hi", "o_lo", "x2_steps", "sq_ready", "x2_gamma"))
        norm2_steps, x2n_steps, x2s_hi, x2s_lo = map(
            sem, ("norm2_steps", "x2n_steps", "x2s_hi", "x2s_lo"))
        tanh_ready, h_steps, h_hi, h_lo = map(sem, ("tanh_ready", "h_steps", "h_hi", "h_lo"))
        x2_kept, x3_steps, x3_tok, ln_steps, ln_scaled, final_steps = map(
            sem, ("x2_kept", "x3_steps", "x3_tok", "ln_steps", "ln_scaled", "final_steps"))


        stage = (work_b, work_d)

        def ktiles(a):
            return a.rearrange("(k p) n -> p k n", p=P)

        chunks = [(ktiles(wqkT), wqk[:, 0], wqk[:, 1]), (ktiles(woT), wo[:, 0], wo[:, 1])]
        sel_v = sel_dram.rearrange("p (h c m) -> h p c m", h=2, c=SEQ)
        chunks += [(sel_v[h], sel[:, SEQ * h:SEQ * h + SEQ], None) for h in range(2)]
        EARLY = len(chunks)
        for k in range(KD):
            for h in range(2):
                cols = slice(HID * h, HID * h + HID)
                chunks.append((ktiles(ghT)[:, k, cols], gh[:, 0, k, cols], gh[:, 1, k, cols]))
        for h in range(2):
            cs = slice(CH // 2 * h, CH // 2 * h + CH // 2)
            chunks.append((ktiles(outT)[:, cs], wout[:, 0, cs], wout[:, 1, cs]))

        def stage_view(n):
            flat = stage[n % 2][:, :, :].rearrange("p a n -> p (a n)")
            shape = chunks[n][1].shape
            flat = flat[:, 0:int(np.prod(shape[1:]))]
            return flat if len(shape) == 2 else flat.rearrange("p (a n) -> p a n", a=shape[1])

        def n_lo(n):
            return sum(c[2] is not None for c in chunks[:n])

        def later(g):
            return not isinstance(g, int) or g > 0

        def table(t, g, m=None):
            if m is not None:
                return tabs[:, t, m, bass.ds(g * SEQ, SEQ)].unsqueeze(2).to_broadcast([P, SEQ, L])
            return tabs[:, t, :, bass.ds(g * SEQ, SEQ)].unsqueeze(3).to_broadcast([P, KD, SEQ, L])

        def by_seq(ap):
            return ap.rearrange("p k (b t) -> p k b t", b=SEQ)

        x_v = x.rearrange("(g c b) t f -> g (b t) c f", g=GROUPS, c=TT)
        out_v = out.rearrange("(g c b) t f -> g (b t) c f", g=GROUPS, c=TT)
        xT_v = xT.rearrange("(k p) (g n) -> g p k n", p=P, g=GROUPS)
        shift_v = shift_dram.rearrange("(g c b) f -> g b c f", g=GROUPS, c=TT)
        passes = [(k, a, b) for a, b in ((0, 0), (1, 0), (0, 1)) for k in range(KD)]


        RS = 2 + 3 * NEWTON
        N1, N2, LN = 2 * TT + 2 + RS, 1 + RS, 2 * TT + 2 + RS
        block = ctx.enter_context(nc.Block())

        @block.sync
        def _(sp):
            def load_stage(n):
                if n >= 2:
                    sp.wait_ge(stage_hi, n - 1)
                    if n_lo(n - 1):
                        sp.wait_ge(stage_lo, n_lo(n - 1))
                sp.dma_start(stage_view(n), chunks[n][0]).then_inc(ld_stage[n % 2], 16)

            def load_x(g):
                if later(g):
                    sp.wait_ge(xt_mm, g)
                sp.dma_start(xtok[:, :, :], x_v[g]).then_inc(ld_x, 16)

            def load_res(g):
                if later(g):
                    sp.wait_ge(x2_steps, 2 * g)
                sp.dma_start(xres[:, :, :], xT_v[g]).then_inc(ld_res, 16)

            def load_shift(f):
                if later(f):
                    sp.wait_ge(final_steps, 2 * f)
                for b in range(2):
                    sp.dma_start(shift[64 * b:64 * b + 64, :, :],
                                 shift_v[f][b:b + 1].to_broadcast([L, TT, D])).then_inc(ld_shift, 16)

            def move_pairs(g):
                sp.wait_ge(k_ready, 3 * g + 1)
                for j in range(J):
                    r = slice(32 * j, 32 * j + 32)
                    sp.dma_start(kpair[r, :, j, :], kTb[r, :, :]).then_inc(kpair_moved, 16)
                sp.wait_ge(q_ready, 3 * g + 1)
                for j in range(J):
                    r = slice(32 * j, 32 * j + 32)
                    sp.dma_start(qpair[r, :, j, :], qT[r, :, :]).then_inc(qpair_moved, 16)

            def store(f):
                sp.wait_ge(final_steps, 2 * f + 2)
                sp.dma_start(out_v[f], final[:, :, :]).then_inc(out_stored, 16)

            load_x(0)
            sp.dma_start(cst[:, :], consts).then_inc(ld_const, 16)
            sp.dma_start(cond, condT).then_inc(ld_const, 16)
            sp.dma_start(tabw, tabT).then_inc(ld_const, 16)
            sp.dma_start(linw, linT).then_inc(ld_const, 16)
            for n in range(2):
                load_stage(n)
            for dst, src in ((lnw_b, lnw), (lnb_b, lnb), (linb_b, linb)):
                sp.dma_start(dst, src.to_broadcast([P, D])).then_inc(ld_const, 16)
            sp.dma_start(outb[:, :], outb_dram).then_inc(ld_const, 16)
            sp.dma_start(wv[:, :, :], ktiles(wvT)).then_inc(ld_const, 16)
            for n in range(2, EARLY):
                load_stage(n)
            sp.wait_ge(setup_dve, SETUP_SHIFT)
            sp.dma_start(shift_dram, cvec[0:B]).then_inc(shift_stored, 16)
            sp.wait_ge(zeroed, ZEROED)
            move_pairs(0)
            load_res(0)
            load_x(1)
            sp.wait_ge(shift_stored, 16)
            for n in range(EARLY, len(chunks)):
                load_stage(n)
            move_pairs(1)

            def step(i, first=False):
                load_x(i + 1)
                load_res(i)
                if first:
                    load_shift(0)
                else:
                    store(i - 2)
                    load_shift(i - 1)
                move_pairs(i + 1)

            step(1, first=True)
            with sp.Fori(2, GROUPS - 1) as i:
                step(i)
            load_res(GROUPS - 1)
            store(GROUPS - 3)
            load_shift(GROUPS - 2)
            store(GROUPS - 2)
            load_shift(GROUPS - 1)
            store(GROUPS - 1)
            sp.wait_ge(out_stored, 16 * GROUPS)

        @block.tensor
        def _(pe):
            mm = nc.tensor.matmul

            def setup():
                pe.wait_ge(ld_const, LD_CONST)
                for t in range(len(TABLES)):
                    for k in range(KD):
                        c = (t * KD + k) * B
                        mm(banks[:, c // 512, c % 512:c % 512 + B], tabw[:, t, P * k:P * k + P], cond,
                           start=True, stop=True)
                mm(banks[0:B, 2, 0:D], cond, linw, start=True, stop=True).then_inc(tables_mm, 1)

            def transpose_x(g):
                pe.wait_ge(xs_scaled, g + 1)
                if later(g):
                    pe.wait_ge(p_ready, 4 * g)
                for k in range(KD):
                    for t in range(TT):
                        last = nc.tensor.transpose(banks[:, 4 + k, P * t:P * t + P],
                                                   xtok[:, t, P * k:P * k + P], ident)
                last.then_inc(xt_mm, 1)

            def project_qk(g, which, done):
                for m in range(G):
                    c = D * which + P * m
                    for n, (k, a, b) in enumerate(passes):
                        if b and m == 0:
                            pe.wait_ge(xs_lo, g + 1)
                        last = mm(banks[:, 4 + m, :], wqk[:, a, k, c:c + P], xs[:, b, k, :],
                                  start=(n == 0), stop=(n == 5))
                last.then_inc(done, 1)

            def k_proj(g):
                pe.wait_ge(xs_hi, g + 1)
                project_qk(g, 1, k_mm)

            def q_proj(g):
                pe.wait_ge(k_ready, 3 * g + 3)
                project_qk(g, 0, q_mm)

            def v_proj(g):
                if later(g):
                    pe.wait_ge(x2_steps, 2 * g)
                for b in range(SEQ):
                    for k in range(KD):
                        for e in range(2):
                            wcols = wv[:, k, :].rearrange("p (j e d) -> p j e d", e=2, d=DH)[:, :, e, :]
                            last = mm(banks[64 * e:64 * e + 64, 6 + b // 4, P * (b % 4):P * (b % 4) + P],
                                      xn[:, k, L * b:L * b + L], wcols, start=(k == 0), stop=(k == KD - 1))
                last.then_inc(v_mm, 1)

            def scores_for_max(g, n):
                if n == 0:
                    pe.wait_ge(v_ready, 2 * g + 2)
                    pe.wait_ge(kpair_moved, 64 * g + 64)
                    pe.wait_ge(q_ready, 3 * g + 3)
                else:
                    pe.wait_ge(max_ready, 4 * g + n - 1)
                h, base = n // 2, 6 - 2 * (n % 2)
                for i in range(4):
                    b = 4 * (n % 2) + i
                    last = mm(banks[:, base + i // 2, 256 * (i % 2):256 * (i % 2) + 256], qpar[:, h, b],
                              kpair[:, h, :, L * b:L * b + L], start=True, stop=True)
                last.then_inc(s_mm, 1)

            def transpose_max(g):
                for e in range(2):
                    r = slice(64 * e, 64 * e + 64)
                    last = nc.tensor.transpose(max_t[r, :], smax[r, :], identb[r, :])
                last.then_inc(mt_mm, 1)

            def scores(g, n):
                h = n // 2
                if n == 0:
                    pe.wait_ge(negmax_ready, g + 1)
                    pe.wait_ge(qpair_moved, 64 * g + 64)
                else:
                    pe.wait_ge(p_ready, 4 * g + n)
                for i in range(4):
                    b = 4 * (n % 2) + i
                    dst = banks[:, 4 + i // 2, 256 * (i % 2):256 * (i % 2) + 256]
                    mm(dst, kpar[:, h, b], qpair[:, h, :, L * b:L * b + L], start=True, stop=False)
                    last = mm(dst, sel[:, SEQ * h + b], negmax[:, :, :], start=False, stop=True)
                last.then_inc(st_mm, 1)

            def attend(g, h):
                pe.wait_ge(p_ready, 4 * g + 2 * h + 2)
                if h:
                    pe.wait_ge(o_steps, 4 * g + 2)
                for j in range(J):
                    last = mm(banks[32 * j:32 * j + 32, 7, :], cst[:, C_BLK:C_BLK + 32], pt[:, :, j, :],
                              start=True, stop=True)
                last.then_inc(den_mm, 1)
                for b in range(SEQ):
                    for j in range(J):
                        last = mm(banks[32 * j:32 * j + 32, 6, L * b:L * b + L], vblk[:, b, J * h + j],
                                  pt[:, b, j, :], start=True, stop=True)
                last.then_inc(o_mm, 1)

            def o_proj(g):
                pe.wait_ge(o_hi, 2 * g + 2)
                pe.wait_ge(o_lo, 2 * g + 2)
                for m in range(KD):
                    for n, (k, a, b) in enumerate(passes):
                        last = mm(banks[:, 6 + m, :], wo[:, a, k, P * m:P * m + P], os_[:, b, k, :],
                                  start=(n == 0), stop=(n == 5))
                last.then_inc(op_mm, 1)

            def square_sums(g):
                pe.wait_ge(sq_ready, g + 1)
                for t in range(TT):
                    for k in range(KD):
                        last = mm(banks[32 * t:32 * t + 32, 0, 0:P], cst[:, C_ONE:C_ONE + 32],
                                  work_c[:, k, P * t:P * t + P], start=(k == 0), stop=(k == KD - 1))
                last.then_inc(ss_mm, 1)

            def spread_rms(g):
                pe.wait_ge(norm2_steps, N2 * g + N2)
                for t in range(TT):
                    last = mm(banks[:, 1, P * t:P * t + P], cst[:, C_ROW + P * t:C_ROW + P * t + P],
                              nt2[:, 1, :], start=True, stop=True)
                last.then_inc(rb_mm, 1)

            def gate_hidden(f, c):
                if c == 0:
                    pe.wait_ge(x2s_hi, f + 1)
                    if later(f):
                        pe.wait_ge(x3_tok, f)
                else:
                    pe.wait_ge(h_steps, 2 * CH * f + 2 * c - 1)
                for part, done in enumerate((gate_mm, hidden_mm)):
                    if c and part:
                        pe.wait_ge(h_steps, 2 * CH * f + 2 * c)
                    w = HID * part + P * c
                    for n, (k, a, b) in enumerate(passes):
                        if c == 0 and part == 0 and n == 4:
                            pe.wait_ge(x2s_lo, f + 1)
                        last = mm(banks[:, 2 + part, :], gh[:, a, k, w:w + P], x2s[:, b, k, :],
                                  start=(n == 0), stop=(n == 5))
                    last.then_inc(done, 1)

            def ffn_out(f, c):
                pe.wait_ge(h_hi, CH * f + c + 1)
                pe.wait_ge(h_lo, CH * f + c + 1)
                for m in range(KD):
                    for a, b in ((0, 0), (1, 0), (0, 1)):
                        last = mm(banks[:, m, :], wout[:, a, c, P * m:P * m + P], hs[:, c % 2, b, :],
                                  start=(c == 0 and a == b == 0), stop=(c == CH - 1 and b == 1))
                last.then_inc(out_mm, 1)

            def transpose_out(f):
                pe.wait_ge(x3_steps, 3 * f + 3)
                for t in range(TT):
                    for k in range(KD):
                        c = 256 * (t % 2) + P * k
                        last = nc.tensor.transpose(banks[:, 2 + t // 2, c:c + P],
                                                   work_d[:, k, P * t:P * t + P], ident)
                last.then_inc(ft_mm, 1)

            def head(g, norm2=True, ln=True):
                k_proj(g)
                if ln:
                    transpose_out(g - 2)
                if norm2:
                    square_sums(g - 1)
                v_proj(g)
                if norm2:
                    spread_rms(g - 1)
                q_proj(g)

            def main(g, fed=True, more=True):
                f = g - 1
                if fed:
                    gate_hidden(f, 0)
                scores_for_max(g, 0)
                scores_for_max(g, 1)
                if fed:
                    gate_hidden(f, 1)
                    ffn_out(f, 0)
                scores_for_max(g, 2)
                scores_for_max(g, 3)
                if fed:
                    gate_hidden(f, 2)
                pe.wait_ge(max_ready, 4 * g + 4)
                if fed:
                    ffn_out(f, 1)
                transpose_max(g)
                if fed:
                    gate_hidden(f, 3)
                scores(g, 0)
                if fed:
                    ffn_out(f, 2)
                    gate_hidden(f, 4)
                scores(g, 1)
                if fed:
                    ffn_out(f, 3)
                attend(g, 0)
                scores(g, 2)
                if fed:
                    gate_hidden(f, 5)
                scores(g, 3)
                if fed:
                    ffn_out(f, 4)
                attend(g, 1)
                if fed:
                    gate_hidden(f, 6)
                if more:
                    transpose_x(g + 1)
                if fed:
                    ffn_out(f, 5)
                    gate_hidden(f, 7)
                o_proj(g)
                if fed:
                    ffn_out(f, 6)
                    ffn_out(f, 7)

            setup()
            transpose_x(0)
            pe.wait_ge(stage_lo, n_lo(EARLY))
            pe.wait_ge(stage_hi, EARLY)
            head(0, norm2=False, ln=False)
            main(0, fed=False)
            head(1, ln=False)
            pe.wait_ge(stage_hi, len(chunks))
            pe.wait_ge(stage_lo, n_lo(len(chunks)))
            main(1)
            head(2)
            with pe.Fori(2, GROUPS - 1) as i:
                main(i)
                head(i + 1)
            main(GROUPS - 1, more=False)
            transpose_out(GROUPS - 2)
            square_sums(GROUPS - 1)
            spread_rms(GROUPS - 1)
            gate_hidden(GROUPS - 1, 0)
            for c in range(1, CH):
                gate_hidden(GROUPS - 1, c)
                ffn_out(GROUPS - 1, c - 1)
            ffn_out(GROUPS - 1, CH - 1)
            transpose_out(GROUPS - 1)

        @block.scalar
        def _(act):
            def cut_hi(n):
                act.wait_ge(ld_stage[n % 2], 16 * (n // 2 + 1))
                nc.scalar.activation(chunks[n][1], stage_view(n), ACT.Copy).then_inc(stage_hi, 1)

            def xs_split(g):
                act.wait_ge(xn_beta, g + 1)
                nc.scalar.activation(xs[:, 0], xn[:, :, :], ACT.Copy).then_inc(xs_hi, 1)

            def k_out(g):
                act.wait_ge(k_mm, g + 1)
                nc.scalar.activation(kTb[:, :, :], banks[:, 4:6, :], ACT.Copy).then_inc(k_ready, 1)
                for e in range(2):
                    nc.scalar.activation(kpar[:, :, :, e, :], by_seq(banks[:, 4:6, :]), ACT.Copy,
                                         scale=cst[:, C_PAR + e:C_PAR + e + 1]).then_inc(k_ready, 1)

            def v_out(g):
                act.wait_ge(v_mm, g + 1)
                for e in range(2):
                    r = slice(64 * e, 64 * e + 64)
                    nc.scalar.activation(vblk[r, :, :, e, :], v_psum[r], ACT.Copy).then_inc(v_ready, 1)

            def tanh(f, c):
                act.wait_ge(gate_mm, CH * f + c + 1)
                if c == 0 and later(f):
                    act.wait_ge(x3_steps, 3 * f)
                if c >= 2 or later(f):
                    act.wait_ge(h_lo, CH * f + c - 1)
                nc.scalar.activation(act_t[:, c % 2, :], banks[:, 2, :], ACT.Tanh, scale=0.5)\
                    .then_inc(tanh_ready, 1)

            def hidden_hi(f, c):
                act.wait_ge(h_steps, 2 * CH * f + 2 * c + 2)
                if c >= 2 or later(f):
                    act.wait_ge(out_mm, CH * f + c - 1)
                nc.scalar.activation(hs[:, c % 2, 0, :], act_t[:, c % 2, :], ACT.Copy).then_inc(h_hi, 1)

            def exp(g, n):
                act.wait_ge(st_mm, 4 * g + n + 1)
                act.wait_ge(o_mm, 2 * g + n // 2)
                b = 4 * (n % 2)
                nc.scalar.activation(pt[:, b:b + 4].rearrange("p b j q -> p (b j q)"),
                                     banks[:, 4:6, :].rearrange("p k n -> p (k n)"), ACT.Exp,
                                     scale=SCALE).then_inc(p_ready, 1)

            def o_split(g, h):
                act.wait_ge(o_steps, 4 * g + 2 * h + 2)
                nc.scalar.activation(os_[:, 0, h, :], work_c[:, 1, :], ACT.Copy).then_inc(o_hi, 1)

            def square(g):
                act.wait_ge(x2_steps, 2 * g + 2)
                act.wait_ge(o_lo, 2 * g + 2)
                nc.scalar.activation(work_c[:, :, :], x2[:, :, :], ACT.Square).then_inc(sq_ready, 1)

            def x2_split(g):
                act.wait_ge(x2n_steps, 2 * g + 2)
                nc.scalar.activation(x2s[:, 0], work_b[:, :, :], ACT.Copy).then_inc(x2s_hi, 1)

            def copy_x3(f):
                act.wait_ge(ft_mm, f + 1)
                if later(f):
                    act.wait_ge(out_stored, 16 * f)
                nc.scalar.activation(final[:, :, :].rearrange("p t n -> p (t n)"),
                                     banks[:, 2:4, :].rearrange("p k n -> p (k n)"), ACT.Copy)\
                    .then_inc(x3_tok, 1)

            def keep_x2(f):
                act.wait_ge(ft_mm, f)
                nc.scalar.activation(work_d[:, :, :], x2[:, :, :], ACT.Copy).then_inc(x2_kept, 1)

            def ln_scale(f):
                act.wait_ge(ln_steps, LN * f + LN)
                for t in range(TT):
                    nc.scalar.activation(final[:, t, :], final[:, t, :], ACT.Identity, scale=nt3[:, 1, t:t + 1],
                                         bias=nt3[:, 3, t:t + 1]).then_inc(ln_scaled, 1)

            def feed(f, c):
                tanh(f, c)
                hidden_hi(f, c)

            def head(g, norm2=True, ln=True):
                k_out(g)
                if ln:
                    copy_x3(g - 2)
                v_out(g)
                if norm2:
                    x2_split(g - 1)
                    keep_x2(g - 1)

            def main(g, fed=True, more=True, ln=True):
                f = g - 1

                def fill(c):
                    if fed:
                        feed(f, c)
                for c in range(4):
                    fill(c)
                exp(g, 0)
                fill(4)
                exp(g, 1)
                if ln:
                    ln_scale(g - 2)
                exp(g, 2)
                o_split(g, 0)
                fill(5)
                exp(g, 3)
                o_split(g, 1)
                fill(6)
                fill(7)
                if more:
                    xs_split(g + 1)
                square(g)

            for n in range(2):
                cut_hi(n)
            act.wait_ge(setup_dve, SETUP_TANH)
            nc.scalar.activation(cvec[0:B], cvec[0:B], ACT.Tanh).then_inc(setup_act, 1)
            for n in range(2, EARLY):
                cut_hi(n)
            xs_split(0)
            act.wait_ge(zeroed, ZEROED)
            head(0, norm2=False, ln=False)
            for n in range(EARLY, len(chunks)):
                cut_hi(n)
            main(0, fed=False, ln=False)
            head(1, ln=False)
            act.wait_ge(shift_stored, 16)
            main(1, ln=False)
            head(2)
            with act.Fori(2, GROUPS - 1) as i:
                main(i)
                head(i + 1)
            main(GROUPS - 1, more=False)
            copy_x3(GROUPS - 2)
            x2_split(GROUPS - 1)
            keep_x2(GROUPS - 1)
            for c in range(CH):
                feed(GROUPS - 1, c)
                if c == 2:
                    ln_scale(GROUPS - 2)
            copy_x3(GROUPS - 1)
            ln_scale(GROUPS - 1)

        @block.vector
        def _(dve):
            V = nc.vector

            def rsqrt(steps, n, v, y, t):
                V.tensor_scalar(y.bitcast(I32), v.bitcast(I32), -0.5, RSQRT_MAGIC, ALU.mult, ALU.add)\
                    .then_inc(steps, 1)
                dve.wait_ge(steps, n + 1)
                V.tensor_scalar(v, v, -0.5, None, ALU.mult).then_inc(steps, 1)
                dve.wait_ge(steps, n + 2)
                for r in range(NEWTON):
                    V.tensor_tensor(t, y, y, ALU.mult).then_inc(steps, 1)
                    dve.wait_ge(steps, n + 3 * r + 3)
                    V.tensor_tensor(t, t, v, ALU.mult).then_inc(steps, 1)
                    dve.wait_ge(steps, n + 3 * r + 4)
                    V.scalar_tensor_tensor(out=y, in0=t, scalar=1.5, in1=y, op0=ALU.add, op1=ALU.mult)\
                        .then_inc(steps, 1)
                    dve.wait_ge(steps, n + 3 * r + 5)

            def setup():
                dve.wait_ge(ld_const, LD_CONST)
                for e in range(2):
                    V.tensor_copy(identb[64 * e:64 * e + 64, :], ident[64 * e:64 * e + 64, 64 * e:64 * e + 64])\
                        .then_inc(identb_ready, 1)
                dve.wait_ge(tables_mm, 1)
                n = len(TABLES) * KD * B
                V.tensor_copy(tabs[:, :, :, :].rearrange("p t k b -> p (t k b)"),
                              banks[:, 0:2, :].rearrange("p k n -> p (k n)")[:, 0:n]).then_inc(tables_ready, 1)
                V.tensor_tensor(cvec[0:B], banks[0:B, 2, 0:D], linb_b[0:B], ALU.add).then_inc(setup_dve, 1)
                V.tensor_tensor(w2[:, :], lnw_b, lnw_b, ALU.mult).then_inc(setup_dve, 1)
                dve.wait_ge(setup_act, 1)
                V.tensor_tensor(cvec[0:B], cvec[0:B], lnb_b[0:B], ALU.add).then_inc(setup_dve, 1)
                dve.wait_ge(setup_dve, 3)
                V.tensor_tensor(cvec[0:B], cvec[0:B], lnw_b[0:B], ALU.mult).then_inc(setup_dve, 1)
                dve.wait_ge(setup_dve, 4)
                V.tensor_tensor(cvec[0:B], cvec[0:B], lnb_b[0:B], ALU.add).then_inc(setup_dve, 1)

            def cut_lo(n):
                if chunks[n][2] is not None:
                    dve.wait_ge(stage_hi, n + 1)
                    V.tensor_tensor(chunks[n][2], stage_view(n), chunks[n][1].bitcast(F32), ALU.subtract)\
                        .then_inc(stage_lo, 1)

            def norm1(g):
                dve.wait_ge(ld_x, 16 * g + 16)
                for t in range(TT):
                    V.bn_stats(stat[:, 0, t, :], xtok[:, t, :]).then_inc(norm1_steps, 1)
                dve.wait_ge(norm1_steps, N1 * g + TT)
                V.memset(nt1[:, 2, :], 0.0)
                for t in range(TT):
                    V.bn_aggr(mv[:, 0, t, :], stat[:, 0, t, :]).then_inc(norm1_steps, 1)
                v, y, t = (nt1[:, i, :] for i in range(3))
                dve.wait_ge(norm1_steps, N1 * g + 2 * TT)
                V.tensor_tensor(t, mv[:, 0, :, 0], mv[:, 0, :, 0], ALU.mult).then_inc(norm1_steps, 1)
                dve.wait_ge(norm1_steps, N1 * g + 2 * TT + 1)
                V.scalar_tensor_tensor(out=v, in0=t, scalar=EPS_RMS, in1=mv[:, 0, :, 1], op0=ALU.add,
                                       op1=ALU.add).then_inc(norm1_steps, 1)
                dve.wait_ge(norm1_steps, N1 * g + 2 * TT + 2)
                rsqrt(norm1_steps, N1 * g + 2 * TT + 2, v, y, t)

            def scale_xn(g):
                dve.wait_ge(xt_mm, g + 1)
                V.tensor_tensor(by_seq(xn[:, :, :]), by_seq(banks[:, 4:6, :]), table(GA, g), ALU.mult)\
                    .then_inc(xn_gamma, 1)

            def q_out(g):
                dve.wait_ge(q_mm, g + 1)
                V.tensor_copy(qT[:, :, :], banks[:, 4:6, :]).then_inc(q_ready, 1)
                dve.wait_ge(q_ready, 3 * g + 1)
                for e in range(2):
                    V.tensor_scalar(qpar[:, :, :, e, :], by_seq(qT[:, :, :]),
                                    cst[:, C_PAR + e:C_PAR + e + 1], None, ALU.mult).then_inc(q_ready, 1)

            def max_over_keys(g, n):
                dve.wait_ge(s_mm, 4 * g + n + 1)
                base = 6 - 2 * (n % 2)
                V.tensor_reduce(smax[:, 16 * n:16 * n + 16],
                                banks[:, base:base + 2, :].rearrange("p k (r c) -> p (k r) c", c=L),
                                AX.X, ALU.max).then_inc(max_ready, 1)

            def negate_max(g):
                dve.wait_ge(mt_mm, g + 1)
                V.tensor_tensor(negmax[:, :, :], max_t.unsqueeze(1).to_broadcast([P, J, L]),
                                cst[:, C_NEG:C_NEG + J].unsqueeze(2).to_broadcast([P, J, L]), ALU.mult)\
                    .then_inc(negmax_ready, 1)

            def normalise(g, h):
                dve.wait_ge(den_mm, 2 * g + h + 1)
                V.reciprocal(work_c[:, 0, :], banks[:, 7, :]).then_inc(o_steps, 1)
                dve.wait_ge(o_steps, 4 * g + 2 * h + 1)
                dve.wait_ge(o_mm, 2 * g + h + 1)
                if h:
                    dve.wait_ge(o_hi, 2 * g + 1)
                    dve.wait_ge(o_lo, 2 * g + 1)
                V.tensor_tensor(work_c[:, 1, :], banks[:, 6, :], work_c[:, 0, :], ALU.mult).then_inc(o_steps, 1)

            def residual1(g):
                dve.wait_ge(op_mm, g + 1)
                dve.wait_ge(ld_res, 16 * g + 16)
                V.tensor_tensor(by_seq(work_b[:, :, :]), by_seq(banks[:, 6:8, :]), table(AA, g), ALU.mult)\
                    .then_inc(x2_steps, 1)
                dve.wait_ge(x2_steps, 2 * g + 1)
                V.tensor_tensor(x2[:, :, :], work_b[:, :, :], xres[:, :, :], ALU.add).then_inc(x2_steps, 1)

            def norm2(g):
                v, y, t = (nt2[:, i, :] for i in range(3))
                dve.wait_ge(ss_mm, g + 1)
                V.tensor_scalar(v, banks[:, 0, 0:P], 1.0 / D, EPS_RMS, ALU.mult, ALU.add).then_inc(norm2_steps, 1)
                dve.wait_ge(norm2_steps, N2 * g + 1)
                rsqrt(norm2_steps, N2 * g + 1, v, y, t)

            def scale_x2(g):
                dve.wait_ge(x2_gamma, g + 1)
                dve.wait_ge(rb_mm, g + 1)
                V.tensor_tensor(work_b[:, :, :], work_b[:, :, :],
                                banks[:, 1, :].unsqueeze(1).to_broadcast([P, KD, TOK]), ALU.mult)\
                    .then_inc(x2n_steps, 1)
                dve.wait_ge(x2n_steps, 2 * g + 1)
                V.tensor_tensor(by_seq(work_b[:, :, :]), by_seq(work_b[:, :, :]), table(BF, g), ALU.add)\
                    .then_inc(x2n_steps, 1)

            def feed(f, c):
                a = act_t[:, c % 2, :]
                dve.wait_ge(tanh_ready, CH * f + c + 1)
                V.scalar_tensor_tensor(out=a, in0=a, scalar=1.0, in1=banks[:, 2, :], op0=ALU.add,
                                       op1=ALU.mult).then_inc(h_steps, 1)
                dve.wait_ge(h_steps, 2 * CH * f + 2 * c + 1)
                dve.wait_ge(hidden_mm, CH * f + c + 1)
                V.scalar_tensor_tensor(out=a, in0=a, scalar=0.5, in1=banks[:, 3, :], op0=ALU.mult,
                                       op1=ALU.mult).then_inc(h_steps, 1)

            def residual2(f):
                dve.wait_ge(out_mm, CH * f + CH)
                for m in range(KD):
                    V.scalar_tensor_tensor(
                        out=act_t[:, m, :].rearrange("p (b t) -> p b t", b=SEQ),
                        in0=banks[:, m, :].rearrange("p (b t) -> p b t", b=SEQ), scalar=outb[:, m:m + 1],
                        in1=table(AF, f, m), op0=ALU.add, op1=ALU.mult).then_inc(x3_steps, 1)
                dve.wait_ge(x3_steps, 3 * f + 2)
                dve.wait_ge(x2_kept, f + 1)
                V.tensor_tensor(work_d[:, :, :], work_d[:, :, :], act_t[:, :, :], ALU.add).then_inc(x3_steps, 1)

            def layernorm(f):
                dve.wait_ge(x3_tok, f + 1)
                for t in range(TT):
                    V.bn_stats(stat[:, 1, t, :], final[:, t, :]).then_inc(ln_steps, 1)
                dve.wait_ge(ln_steps, LN * f + TT)
                V.memset(nt3[:, 2, :], 0.0)
                for t in range(TT):
                    V.bn_aggr(mv[:, 1, t, :], stat[:, 1, t, :]).then_inc(ln_steps, 1)
                v, y, t, nb = (nt3[:, i, :] for i in range(4))
                dve.wait_ge(ln_steps, LN * f + 2 * TT)
                V.tensor_scalar(v, mv[:, 1, :, 1], EPS_LN, None, ALU.add).then_inc(ln_steps, 1)
                dve.wait_ge(ln_steps, LN * f + 2 * TT + 1)
                rsqrt(ln_steps, LN * f + 2 * TT + 1, v, y, t)
                V.scalar_tensor_tensor(out=nb, in0=mv[:, 1, :, 0], scalar=-1.0, in1=y, op0=ALU.mult,
                                       op1=ALU.mult).then_inc(ln_steps, 1)

            def head(g, norm2_=True):
                if norm2_:
                    norm2(g - 1)
                if norm2_:
                    scale_x2(g - 1)
                q_out(g)

            def main(g, fed=True, more=True, ln=True):
                f = g - 1

                def fill(c):
                    if fed:
                        feed(f, c)
                fill(0)
                max_over_keys(g, 0)
                max_over_keys(g, 1)
                fill(1)
                max_over_keys(g, 2)
                max_over_keys(g, 3)
                fill(2)
                negate_max(g)
                fill(3)
                fill(4)
                if ln:
                    layernorm(g - 2)
                normalise(g, 0)
                fill(5)
                if more:
                    norm1(g + 1)
                normalise(g, 1)
                fill(6)
                if more:
                    scale_xn(g + 1)
                fill(7)
                residual1(g)
                if fed:
                    residual2(f)

            norm1(0)
            setup()
            for n in range(EARLY):
                cut_lo(n)
            scale_xn(0)
            head(0, norm2_=False)
            for n in range(EARLY, len(chunks)):
                cut_lo(n)
            main(0, fed=False, ln=False)
            head(1)
            main(1, ln=False)
            head(2)
            with dve.Fori(2, GROUPS - 1) as i:
                main(i)
                head(i + 1)
            main(GROUPS - 1, more=False)
            norm2(GROUPS - 1)
            scale_x2(GROUPS - 1)
            for c in range(CH):
                feed(GROUPS - 1, c)
                if c == 1:
                    layernorm(GROUPS - 2)
            residual2(GROUPS - 1)
            layernorm(GROUPS - 1)

        @block.gpsimd
        def _(pool):
            tt = nc.gpsimd.tensor_tensor

            def scale_x(g):
                pool.wait_ge(norm1_steps, N1 * g + N1)
                tt(xtok[:, :, :], xtok[:, :, :], nt1[:, 1, :].unsqueeze(2).to_broadcast([P, TT, D]),
                   ALU.mult).then_inc(xs_scaled, 1)

            def shift_xn(g):
                pool.wait_ge(xn_gamma, g + 1)
                tt(by_seq(xn[:, :, :]), by_seq(xn[:, :, :]), table(BA, g), ALU.add).then_inc(xn_beta, 1)

            def xs_split(g):
                pool.wait_ge(xs_hi, g + 1)
                tt(xs[:, 1], xn[:, :, :], xs[:, 0].bitcast(F32), ALU.subtract).then_inc(xs_lo, 1)

            def o_split(g, h):
                pool.wait_ge(o_hi, 2 * g + h + 1)
                tt(os_[:, 1, h, :], work_c[:, 1, :], os_[:, 0, h, :].bitcast(F32), ALU.subtract).then_inc(o_lo, 1)

            def x2_by_gamma(g):
                pool.wait_ge(x2_steps, 2 * g + 2)
                tt(by_seq(work_b[:, :, :]), by_seq(x2[:, :, :]), table(GF, g), ALU.mult).then_inc(x2_gamma, 1)

            def x2_split(g):
                pool.wait_ge(x2s_hi, g + 1)
                tt(x2s[:, 1], work_b[:, :, :], x2s[:, 0].bitcast(F32), ALU.subtract).then_inc(x2s_lo, 1)

            def hidden_lo(f, c):
                pool.wait_ge(h_hi, CH * f + c + 1)
                tt(hs[:, c % 2, 1, :], act_t[:, c % 2, :], hs[:, c % 2, 0, :].bitcast(F32), ALU.subtract)\
                    .then_inc(h_lo, 1)

            def finish(f):
                pool.wait_ge(ln_scaled, TT * f + TT)
                pool.wait_ge(ld_shift, 32 * f + 32)
                tt(final[:, :, :], final[:, :, :], w2[:, :].unsqueeze(1).to_broadcast([P, TT, D]), ALU.mult)\
                    .then_inc(final_steps, 1)
                pool.wait_ge(final_steps, 2 * f + 1)
                tt(final[:, :, :], final[:, :, :], shift[:, :, :], ALU.add).then_inc(final_steps, 1)

            def head(g):
                x2_split(g - 1)

            def main(g, fed=True, more=True, ln=True):
                f = g - 1

                def fill(c):
                    if fed:
                        hidden_lo(f, c)
                fill(0)
                fill(1)
                fill(2)
                fill(3)
                fill(4)
                if ln:
                    finish(g - 2)
                o_split(g, 0)
                fill(5)
                if more:
                    scale_x(g + 1)
                o_split(g, 1)
                fill(6)
                if more:
                    shift_xn(g + 1)
                fill(7)
                if more:
                    xs_split(g + 1)
                x2_by_gamma(g)

            nc.gpsimd.memset(vblk[:, :, :, :, :], 0.0).then_inc(zeroed, 1)
            nc.gpsimd.memset(kpair[:, :, :, :], 0.0).then_inc(zeroed, 1)
            nc.gpsimd.memset(qpair[:, :, :, :], 0.0).then_inc(zeroed, 1)
            scale_x(0)
            pool.wait_ge(tables_ready, 1)
            shift_xn(0)
            xs_split(0)
            main(0, fed=False, ln=False)
            head(1)
            main(1, ln=False)
            head(2)
            with pool.Fori(2, GROUPS - 1) as i:
                main(i)
                head(i + 1)
            main(GROUPS - 1, more=False)
            x2_split(GROUPS - 1)
            for c in range(CH):
                hidden_lo(GROUPS - 1, c)
                if c == 3:
                    finish(GROUPS - 2)
            finish(GROUPS - 1)


def kernel(x, cond_256, L1_cond_weight, L1_cond_bias, L1_cond_lin_w, L1_cond_lin_b, **w):
    import concourse.bacc as bacc
    from concourse.bass_utils import run_bass_kernel_spmd

    def layer0(name):
        return np.asarray(w["L0_cond_" + name])

    x = np.asarray(x)
    consts, sel = shape_constants()
    arrays = dict(
        x=x,
        xT=x.reshape(B * L, D).T,
        condT=np.asarray(cond_256).T,
        tabT=np.stack([layer0(t + "_w").T for t in TABLES], axis=1),
        linT=np.asarray(L1_cond_lin_w).T,
        linb=np.asarray(L1_cond_lin_b).reshape(1, D),
        lnw=np.asarray(L1_cond_weight).reshape(1, D),
        lnb=np.asarray(L1_cond_bias).reshape(1, D),
        wqkT=np.concatenate([layer0("W_q").T, layer0("W_k").T], axis=1),
        wvT=layer0("W_v").T,
        woT=layer0("W_o").T,
        ghT=np.concatenate([layer0("gate_w").T, layer0("hidden_w").T], axis=1),
        outT=layer0("out_w").T,
        outb=layer0("out_b").reshape(KD, P).T,
        consts=consts,
        sel=sel,
    )
    arrays = {k + "_in": np.ascontiguousarray(a) for k, a in arrays.items()}
    nc = bacc.Bacc("TRN2", target_bir_lowering=False, num_devices=1)
    args = [nc.dram_tensor(k, a.shape, mybir.dt.from_np(a.dtype), kind="ExternalInput").ap()
            for k, a in arrays.items()]
    args.append(nc.dram_tensor("y", (B, L, D), F32, kind="ExternalOutput").ap())
    build(nc, *args)
    r = run_bass_kernel_spmd(nc, [arrays], core_ids=[0])
    return r.results[0]["y"]
```

```python
from contextlib import ExitStack

import numpy as np

import concourse.bass as bass
from concourse import mybir

F32, F32R, BF16, I32 = mybir.dt.float32, mybir.dt.float32r, mybir.dt.bfloat16, mybir.dt.int32
ALU, ACT, AX = mybir.AluOpType, mybir.ActivationFunctionType, mybir.AxisListType

P = 128
B, L, D = 64, 64, 256
HEADS, DH = 16, 16
DT = 64
HID = 4 * D
KD = D // P
SEQ = 8
TOK = SEQ * L
GROUPS = B // SEQ
TT = TOK // P
G = 2
J = 4
CH = HID // P
SCALE = (HEADS / D) ** 0.5
EPS_RMS, EPS_LN = 1e-6, 1e-5
NEWTON = 3
LD_TABLE = 16 * 3
LD_SHIFT = 16 * 5
SETUP_TANH, SETUP_SHIFT = 1, 5
ZEROED = 3
RSQRT_MAGIC = float(0x5F3759DF)
TABLES = ("attn_gamma", "attn_beta", "attn_alpha", "ffn_gamma", "ffn_beta", "ffn_alpha")
GA, BA, AA, GF, BF, AF = range(6)

C_ID, C_PAR, C_NEG, C_BLK, C_ONE, C_ROW, C_SEL = 0, 128, 130, 134, 166, 198, 202
C_END = C_SEL + G * SEQ * 2


def shape_constants():
    c = np.zeros((P, C_END), np.float32)
    p = np.arange(P)
    c[p, C_ID + p] = 1
    c[p, C_PAR + (p // DH) % 2] = 1
    c[p, C_NEG + p % J] = -1
    for e in range(2):
        c[64 * e:64 * e + 64, C_BLK + DH * e:C_BLK + DH * e + DH] = 1
    c[:, C_ONE:C_ONE + 32] = 1
    for t in range(TT):
        c[32 * t, C_ROW + t] = 1
    for r in range(P):
        c[r, C_SEL + 2 * ((r % 64) // J) + r // 64] = 1
    return c


def build(nc, x, xT, condT, tabT, linT, linb, lnw, lnb, wqkT, wvT, woT, ghT, outT, outb_dram,
          consts, out):
    with ExitStack() as ctx:
        def sb(name, shape, dt=F32):
            return ctx.enter_context(nc.sbuf_tensor(name, shape, dt))

        def sem(name):
            return ctx.enter_context(nc.semaphore(name))

        cst = sb("cst", [P, C_END])
        sel = sb("sel", [P, G * SEQ, P], BF16)
        row = sb("row", [P, TT, P])
        identb = sb("identb", [P, 64], BF16)
        wqk = sb("wqk", [P, 2, KD, 2 * D], F32R)
        wv = sb("wv", [P, KD, D])
        wo = sb("wo", [P, 2, KD, D], F32R)
        gh = sb("gh", [P, 2, KD, 2 * HID], F32R)
        wout = sb("wout", [P, 2, CH, D], F32R)
        outb = sb("outb", [P, KD])
        tabs = sb("tabs", [P, len(TABLES), KD, B])
        w2 = sb("w2", [P, D])
        xtok = sb("xtok", [P, TT, D])
        xres = sb("xres", [P, KD, TOK])
        xn = sb("xn", [P, KD, TOK])
        xs = sb("xs", [P, 2, KD, TOK], F32R)
        qT = sb("qT", [P, G, TOK])
        kTb = sb("kTb", [P, G, TOK], BF16)
        qpar = sb("qpar", [P, G, SEQ, 2, L], BF16)
        kpar = sb("kpar", [P, G, SEQ, 2, L])
        qpair = sb("qpair", [P, G, J, TOK])
        kpair = sb("kpair", [P, G, J, TOK], BF16)
        vblk = sb("vblk", [P, SEQ, G * J, 2, DH])
        smax = sb("smax", [P, G * SEQ * J], BF16)
        negmax = sb("negmax", [P, J, L], BF16)
        pt = sb("pt", [P, SEQ, J, L])
        work_b = sb("work_b", [P, KD, TOK])
        work_c = sb("work_c", [P, 2, TOK])
        work_d = sb("work_d", [P, KD, TOK])
        os_ = sb("os", [P, 2, G, TOK], F32R)
        x2 = sb("x2", [P, KD, TOK])
        x2s = sb("x2s", [P, 2, KD, TOK], F32R)
        act_t = sb("act_t", [P, 2, TOK])
        hs = sb("hs", [P, 2, 2, TOK], F32R)
        final = sb("final", [P, TT, D])
        shift = sb("shift", [P, TT, D])
        stat = sb("stat", [P, 2, TT, 6])
        mv = sb("mv", [P, 2, TT, 2])
        nt1 = sb("nt1", [P, 3, 2, TT])
        nt2 = sb("nt2", [P, 3, P])
        banks = ctx.enter_context(nc.psum_tensor("banks", [P, 8, 512], F32))
        shift_dram = nc.dram_tensor("shift_dram", [B, D], F32, kind="Internal").ap()

        ident = cst[:, C_ID:C_ID + P]
        setup_area = pt[0:DT].rearrange("p b j q -> p (b j q)")
        n_tab = len(TABLES) * D
        tabw = setup_area[:, 0:n_tab].rearrange("p (t n) -> p t n", n=D)
        linw = setup_area[:, n_tab:n_tab + D]
        cond = setup_area[:, n_tab + D:n_tab + D + B]
        lnw_b, lnb_b, linb_b = final[:, 0, :], final[:, 1, :], final[:, 2, :]
        cvec = final[:, 3, :]
        v_psum = banks[:, 6:8, :].rearrange("p k (b j d) -> p (k b) j d", b=4, d=DH)
        max_t = banks[:, 6, :].bitcast(BF16)[:, 0:L]


        ld_tables, ld_wv, ld_lin, ld_x, ld_res, ld_shift = map(
            sem, ("ld_tables", "ld_wv", "ld_lin", "ld_x", "ld_res", "ld_shift"))
        ld_stage = (sem("ld_stage0"), sem("ld_stage1"))
        kpair_moved, qpair_moved, out_stored, shift_stored = map(
            sem, ("kpair_moved", "qpair_moved", "out_stored", "shift_stored"))
        zeroed, selectors_ready = sem("zeroed"), sem("selectors_ready")
        tables_mm, shift_mm, tables_ready, identb_ready, setup_dve, setup_act = map(
            sem, ("tables_mm", "shift_mm", "tables_ready", "identb_ready", "setup_dve", "setup_act"))
        stage_hi, stage_lo = sem("stage_hi"), sem("stage_lo")
        k_mm, q_mm, v_mm, s_mm, mt_mm, st_mm, den_mm, o_mm, xt_mm, op_mm, ss_mm, rb_mm, gate_mm, hidden_mm, out_mm, ft_mm = map(
            sem, ("k_mm", "q_mm", "v_mm", "s_mm", "mt_mm", "st_mm", "den_mm", "o_mm", "xt_mm", "op_mm", "ss_mm",
                  "rb_mm", "gate_mm", "hidden_mm", "out_mm", "ft_mm"))
        k_ready, q_ready, v_ready, max_ready, negmax_ready, p_ready = map(
            sem, ("k_ready", "q_ready", "v_ready", "max_ready", "negmax_ready", "p_ready"))
        nt1_set, x_stats, norm1_steps, xs_scaled, xn_gamma, xn_beta, xs_hi, xs_lo = map(
            sem, ("nt1_set", "x_stats", "norm1_steps", "xs_scaled", "xn_gamma", "xn_beta", "xs_hi", "xs_lo"))
        o_steps, o_hi, o_lo, x2_steps, sq_ready, x2_gamma = map(
            sem, ("o_steps", "o_hi", "o_lo", "x2_steps", "sq_ready", "x2_gamma"))
        norm2_steps, x2n_steps, x2s_hi, x2s_lo = map(
            sem, ("norm2_steps", "x2n_steps", "x2s_hi", "x2s_lo"))
        tanh_ready, h_steps, h_hi, h_lo = map(sem, ("tanh_ready", "h_steps", "h_hi", "h_lo"))
        x2_kept, x3_steps, x3_tok, ln_stats, final_steps = map(
            sem, ("x2_kept", "x3_steps", "x3_tok", "ln_stats", "final_steps"))


        stage = (work_b, work_d)

        def ktiles(a):
            return a.rearrange("(k p) n -> p k n", p=P)

        chunks = [(ktiles(wqkT), wqk[:, 0], wqk[:, 1]), (ktiles(woT), wo[:, 0], wo[:, 1])]
        EARLY = len(chunks)
        for k in range(KD):
            for h in range(2):
                cols = slice(HID * h, HID * h + HID)
                chunks.append((ktiles(ghT)[:, k, cols], gh[:, 0, k, cols], gh[:, 1, k, cols]))
        for h in range(2):
            cs = slice(CH // 2 * h, CH // 2 * h + CH // 2)
            chunks.append((ktiles(outT)[:, cs], wout[:, 0, cs], wout[:, 1, cs]))

        def stage_view(n):
            flat = stage[n % 2][:, :, :].rearrange("p a n -> p (a n)")
            shape = chunks[n][1].shape
            flat = flat[:, 0:int(np.prod(shape[1:]))]
            return flat if len(shape) == 2 else flat.rearrange("p (a n) -> p a n", a=shape[1])

        def cut_in_slot(c):
            return range(EARLY + 2 * (c - 3), EARLY + 2 * (c - 2)) if 3 <= c <= 5 else ()

        def later(g):
            return not isinstance(g, int) or g > 0

        def table(t, g, m=None):
            if m is not None:
                return tabs[:, t, m, bass.ds(g * SEQ, SEQ)].unsqueeze(2).to_broadcast([P, SEQ, L])
            return tabs[:, t, :, bass.ds(g * SEQ, SEQ)].unsqueeze(3).to_broadcast([P, KD, SEQ, L])

        def by_seq(ap):
            return ap.rearrange("p k (b t) -> p k b t", b=SEQ)

        def by_token(ap):
            return ap.rearrange("p (b t) -> p b t", b=SEQ)

        x_v = x.rearrange("(g c b) t f -> g (b t) c f", g=GROUPS, c=TT)
        out_v = out.rearrange("(g c b) t f -> g (b t) c f", g=GROUPS, c=TT)
        xT_v = xT.rearrange("(k p) (g n) -> g p k n", p=P, g=GROUPS)
        shift_v = shift_dram.rearrange("(g c b) f -> g b c f", g=GROUPS, c=TT)
        passes = [(k, a, b) for a, b in ((0, 0), (1, 0), (0, 1)) for k in range(KD)]


        RS = 1 + 3 * NEWTON
        N2 = 1 + RS
        XS, LS = 2 * TT + 2, 2 * TT + 1
        X3, FS = 2 * KD, 2 * TT
        block = ctx.enter_context(nc.Block())

        @block.sync
        def _(sp):
            def load_stage(n):
                if n >= 2:
                    sp.wait_ge(stage_hi, n - 1)
                    sp.wait_ge(stage_lo, n - 1)
                sp.dma_start(stage_view(n), chunks[n][0]).then_inc(ld_stage[n % 2], 16)

            def load_x(g):
                if later(g):
                    sp.wait_ge(xt_mm, g)
                sp.dma_start(xtok[:, :, :], x_v[g]).then_inc(ld_x, 16)

            def load_res(g):
                if later(g):
                    sp.wait_ge(x2_steps, 2 * g)
                sp.dma_start(xres[:, :, :], xT_v[g]).then_inc(ld_res, 16)

            def load_shift(f):
                if later(f):
                    sp.wait_ge(final_steps, FS * f)
                for b in range(2):
                    sp.dma_start(shift[64 * b:64 * b + 64, :, :],
                                 shift_v[f][b:b + 1].to_broadcast([L, TT, D])).then_inc(ld_shift, 16)

            def move_pairs(g):
                sp.wait_ge(k_ready, 3 * g + 1)
                for j in range(J):
                    r = slice(32 * j, 32 * j + 32)
                    sp.dma_start(kpair[r, :, j, :], kTb[r, :, :]).then_inc(kpair_moved, 16)
                sp.wait_ge(q_ready, 3 * g + 1)
                for j in range(J):
                    r = slice(32 * j, 32 * j + 32)
                    sp.dma_start(qpair[r, :, j, :], qT[r, :, :]).then_inc(qpair_moved, 16)

            def store(f):
                sp.wait_ge(final_steps, FS * f + FS)
                sp.dma_start(out_v[f], final[:, :, :]).then_inc(out_stored, 16)

            load_x(0)
            sp.dma_start(tabw, tabT).then_inc(ld_tables, 16)
            sp.dma_start(cond, condT).then_inc(ld_tables, 16)
            sp.dma_start(cst[:, :], consts).then_inc(ld_tables, 16)
            load_stage(0)
            sp.dma_start(wv[:, :, :], ktiles(wvT)).then_inc(ld_wv, 16)
            sp.dma_start(linw, linT).then_inc(ld_lin, 16)
            for dst, src in ((lnw_b, lnw), (lnb_b, lnb), (linb_b, linb)):
                sp.dma_start(dst, src.to_broadcast([P, D])).then_inc(ld_lin, 16)
            sp.dma_start(outb[:, :], outb_dram).then_inc(ld_lin, 16)
            for n in range(1, EARLY + 2):
                load_stage(n)
            sp.wait_ge(setup_dve, SETUP_SHIFT)
            sp.dma_start(shift_dram, cvec[0:B]).then_inc(shift_stored, 16)
            sp.wait_ge(zeroed, ZEROED)
            move_pairs(0)
            load_x(1)
            load_stage(EARLY + 2)
            load_stage(EARLY + 3)
            load_res(0)
            sp.wait_ge(shift_stored, 16)
            for n in range(EARLY + 4, len(chunks)):
                load_stage(n)
            move_pairs(1)

            def step(i, first=False):
                load_x(i + 1)
                load_res(i)
                if first:
                    load_shift(0)
                else:
                    store(i - 2)
                    load_shift(i - 1)
                move_pairs(i + 1)

            step(1, first=True)
            with sp.Fori(2, GROUPS - 1) as i:
                step(i)
            load_res(GROUPS - 1)
            store(GROUPS - 3)
            load_shift(GROUPS - 2)
            store(GROUPS - 2)
            load_shift(GROUPS - 1)
            for h in range(2):
                tiles = slice(TT // 2 * h, TT // 2 * h + TT // 2)
                sp.wait_ge(final_steps, FS * (GROUPS - 1) + TT + TT // 2 * (h + 1))
                sp.dma_start(out_v[GROUPS - 1][:, tiles], final[:, tiles, :]).then_inc(out_stored, 16)
            sp.wait_ge(out_stored, 16 * (GROUPS + 1))

        @block.tensor
        def _(pe):
            mm = nc.tensor.matmul

            def setup_tables():
                pe.wait_ge(ld_tables, LD_TABLE)
                for t in range(len(TABLES)):
                    for k in range(KD):
                        c = (t * KD + k) * B
                        last = mm(banks[:, c // 512, c % 512:c % 512 + B], tabw[:, t, P * k:P * k + P], cond,
                                  start=True, stop=True)
                last.then_inc(tables_mm, 1)

            def setup_shift():
                pe.wait_ge(ld_lin, LD_SHIFT)
                mm(banks[0:B, 2, 0:D], cond, linw, start=True, stop=True).then_inc(shift_mm, 1)

            def transpose_x(g):
                pe.wait_ge(xs_scaled, g + 1)
                if later(g):
                    pe.wait_ge(p_ready, 4 * g)
                for k in range(KD):
                    for t in range(TT):
                        last = nc.tensor.transpose(banks[:, 4 + k, P * t:P * t + P],
                                                   xtok[:, t, P * k:P * k + P], ident)
                last.then_inc(xt_mm, 1)

            def project_qk(g, which, done):
                for m in range(G):
                    c = D * which + P * m
                    for n, (k, a, b) in enumerate(passes):
                        if b and m == 0:
                            pe.wait_ge(xs_lo, g + 1)
                        last = mm(banks[:, 4 + m, :], wqk[:, a, k, c:c + P], xs[:, b, k, :],
                                  start=(n == 0), stop=(n == 5))
                last.then_inc(done, 1)

            def k_proj(g):
                pe.wait_ge(xs_hi, g + 1)
                project_qk(g, 1, k_mm)

            def q_proj(g):
                pe.wait_ge(k_ready, 3 * g + 3)
                project_qk(g, 0, q_mm)

            def v_proj(g):
                if later(g):
                    pe.wait_ge(x2_steps, 2 * g)
                    pe.wait_ge(norm2_steps, N2 * (g - 1) + 1)
                for b in range(SEQ):
                    for k in range(KD):
                        for e in range(2):
                            wcols = wv[:, k, :].rearrange("p (j e d) -> p j e d", e=2, d=DH)[:, :, e, :]
                            last = mm(banks[64 * e:64 * e + 64, 6 + b // 4, P * (b % 4):P * (b % 4) + P],
                                      xn[:, k, L * b:L * b + L], wcols, start=(k == 0), stop=(k == KD - 1))
                last.then_inc(v_mm, 1)

            def scores_for_max(g, n):
                if n == 0:
                    pe.wait_ge(v_ready, 2 * g + 2)
                    pe.wait_ge(kpair_moved, 64 * g + 64)
                    pe.wait_ge(q_ready, 3 * g + 3)
                else:
                    pe.wait_ge(max_ready, 4 * g + n - 1)
                h, base = n // 2, 6 - 2 * (n % 2)
                for i in range(4):
                    b = 4 * (n % 2) + i
                    last = mm(banks[:, base + i // 2, 256 * (i % 2):256 * (i % 2) + 256], qpar[:, h, b],
                              kpair[:, h, :, L * b:L * b + L], start=True, stop=True)
                last.then_inc(s_mm, 1)

            def transpose_max(g):
                for e in range(2):
                    r = slice(64 * e, 64 * e + 64)
                    last = nc.tensor.transpose(max_t[r, :], smax[r, :], identb[r, :])
                last.then_inc(mt_mm, 1)

            def scores(g, n, alternate=False):
                h, base = n // 2, 2 if alternate and n % 2 else 4
                if n == 0:
                    pe.wait_ge(negmax_ready, g + 1)
                    pe.wait_ge(qpair_moved, 64 * g + 64)
                elif not alternate:
                    pe.wait_ge(p_ready, 4 * g + n)
                elif n >= 2:
                    pe.wait_ge(p_ready, 4 * g + n - 1)
                for i in range(4):
                    b = 4 * (n % 2) + i
                    dst = banks[:, base + i // 2, 256 * (i % 2):256 * (i % 2) + 256]
                    mm(dst, kpar[:, h, b], qpair[:, h, :, L * b:L * b + L], start=True, stop=False)
                    last = mm(dst, sel[:, SEQ * h + b], negmax[:, :, :], start=False, stop=True)
                last.then_inc(st_mm, 1)

            def attend(g, h):
                pe.wait_ge(p_ready, 4 * g + 2 * h + 2)
                if h:
                    pe.wait_ge(o_steps, 4 * g + 2)
                for j in range(J):
                    last = mm(banks[32 * j:32 * j + 32, 7, :], cst[:, C_BLK:C_BLK + 32], pt[:, :, j, :],
                              start=True, stop=True)
                last.then_inc(den_mm, 1)
                for b in range(SEQ):
                    for j in range(J):
                        last = mm(banks[32 * j:32 * j + 32, 6, L * b:L * b + L], vblk[:, b, J * h + j],
                                  pt[:, b, j, :], start=True, stop=True)
                last.then_inc(o_mm, 1)

            def o_proj(g):
                pe.wait_ge(o_hi, 2 * g + 2)
                pe.wait_ge(o_lo, 2 * g + 2)
                for m in range(KD):
                    for n, (k, a, b) in enumerate(passes):
                        last = mm(banks[:, 6 + m, :], wo[:, a, k, P * m:P * m + P], os_[:, b, k, :],
                                  start=(n == 0), stop=(n == 5))
                last.then_inc(op_mm, 1)

            def square_sums(g):
                pe.wait_ge(sq_ready, g + 1)
                for t in range(TT):
                    for k in range(KD):
                        last = mm(banks[32 * t:32 * t + 32, 7, 0:P], cst[:, C_ONE:C_ONE + 32],
                                  work_c[:, k, P * t:P * t + P], start=(k == 0), stop=(k == KD - 1))
                last.then_inc(ss_mm, 1)

            def spread_rms(g):
                pe.wait_ge(norm2_steps, N2 * g + N2)
                if later(g):
                    pe.wait_ge(x3_steps, X3 * g - KD)
                for t in range(TT):
                    last = mm(banks[:, 1, P * t:P * t + P], row[:, t, :], nt2[:, 1, :], start=True, stop=True)
                last.then_inc(rb_mm, 1)

            def gate_hidden(f, c, alternate=False):
                base, back = (2 + 2 * (c % 2), 2) if alternate else (2, 1)
                if c == 0:
                    pe.wait_ge(x2s_hi, KD * f + 1)
                    if later(f):
                        pe.wait_ge(x3_tok, f)
                elif c >= back:
                    pe.wait_ge(h_steps, 2 * CH * f + 2 * (c - back) + 1)
                steps = [(part, n) for part in range(2) for n in range(6)]
                if c == 0:
                    steps.sort(key=lambda step: step[1] >= 4)
                for part, n in steps:
                    k, a, b = passes[n]
                    if c >= back and part and n == 0:
                        pe.wait_ge(h_steps, 2 * CH * f + 2 * (c - back) + 2)
                    if c == 0 and part == 0 and n == 1:
                        pe.wait_ge(x2s_hi, KD * f + KD)
                    if c == 0 and part == 0 and n >= 4:
                        pe.wait_ge(x2s_lo, KD * f + k + 1)
                    w = HID * part + P * c
                    last = mm(banks[:, base + part, :], gh[:, a, k, w:w + P], x2s[:, b, k, :],
                              start=(n == 0), stop=(n == 5))
                    if n == 5:
                        last.then_inc((gate_mm, hidden_mm)[part], 1)

            def ffn_out(f, c):
                pe.wait_ge(h_hi, CH * f + c + 1)
                pe.wait_ge(h_lo, CH * f + c + 1)
                for m in range(KD):
                    for a, b in ((0, 0), (1, 0), (0, 1)):
                        last = mm(banks[:, m, :], wout[:, a, c, P * m:P * m + P], hs[:, c % 2, b, :],
                                  start=(c == 0 and a == b == 0), stop=(c == CH - 1 and b == 1))
                last.then_inc(out_mm, 1)

            def transpose_out(f):
                for k in range(KD):
                    pe.wait_ge(x3_steps, X3 * f + KD + k + 1)
                    for t in range(TT):
                        c = 256 * (t % 2) + P * k
                        last = nc.tensor.transpose(banks[:, 2 + t // 2, c:c + P],
                                                   work_d[:, k, P * t:P * t + P], ident)
                last.then_inc(ft_mm, 1)

            def head(g, norm2=True, ln=True):
                if ln:
                    square_sums(g - 1)
                k_proj(g)
                if ln:
                    ffn_out(g - 2, CH - 1)
                elif norm2:
                    square_sums(g - 1)
                v_proj(g)
                if norm2:
                    spread_rms(g - 1)
                if ln:
                    transpose_out(g - 2)
                q_proj(g)

            def main(g, fed=True, more=True):
                f = g - 1
                if fed:
                    gate_hidden(f, 0)
                scores_for_max(g, 0)
                scores_for_max(g, 1)
                if fed:
                    gate_hidden(f, 1)
                    ffn_out(f, 0)
                scores_for_max(g, 2)
                scores_for_max(g, 3)
                if fed:
                    gate_hidden(f, 2)
                pe.wait_ge(max_ready, 4 * g + 4)
                if fed:
                    ffn_out(f, 1)
                transpose_max(g)
                if fed:
                    gate_hidden(f, 3)
                    scores(g, 0)
                    ffn_out(f, 2)
                    gate_hidden(f, 4)
                    scores(g, 1)
                    ffn_out(f, 3)
                    attend(g, 0)
                    scores(g, 2)
                    gate_hidden(f, 5)
                    scores(g, 3)
                    ffn_out(f, 4)
                    attend(g, 1)
                    gate_hidden(f, 6)
                else:
                    for n in range(3):
                        scores(g, n, alternate=True)
                    attend(g, 0)
                    scores(g, 3, alternate=True)
                    attend(g, 1)
                if more:
                    transpose_x(g + 1)
                if fed:
                    ffn_out(f, 5)
                o_proj(g)
                if fed:
                    gate_hidden(f, 7)
                    ffn_out(f, 6)

            setup_tables()
            transpose_x(0)
            setup_shift()
            pe.wait_ge(ld_wv, 16)
            pe.wait_ge(stage_lo, 1)
            pe.wait_ge(stage_hi, 1)
            head(0, norm2=False, ln=False)
            pe.wait_ge(selectors_ready, 2)
            pe.wait_ge(identb_ready, 2)
            main(0, fed=False)
            head(1, ln=False)
            pe.wait_ge(stage_hi, len(chunks))
            pe.wait_ge(stage_lo, len(chunks))
            main(1)
            head(2)
            with pe.Fori(2, GROUPS - 1) as i:
                main(i)
                head(i + 1)
            main(GROUPS - 1, more=False)
            square_sums(GROUPS - 1)
            ffn_out(GROUPS - 2, CH - 1)
            spread_rms(GROUPS - 1)
            transpose_out(GROUPS - 2)
            for c in range(2):
                gate_hidden(GROUPS - 1, c, alternate=True)
            for c in range(2, CH):
                gate_hidden(GROUPS - 1, c, alternate=True)
                ffn_out(GROUPS - 1, c - 2)
            for c in range(CH - 2, CH):
                ffn_out(GROUPS - 1, c)
            transpose_out(GROUPS - 1)

        @block.scalar
        def _(act):
            def cut_hi(n):
                act.wait_ge(ld_stage[n % 2], 16 * (n // 2 + 1))
                nc.scalar.activation(chunks[n][1], stage_view(n), ACT.Copy).then_inc(stage_hi, 1)

            def xs_split(g):
                act.wait_ge(xn_beta, g + 1)
                nc.scalar.activation(xs[:, 0], xn[:, :, :], ACT.Copy).then_inc(xs_hi, 1)

            def k_out(g):
                act.wait_ge(k_mm, g + 1)
                nc.scalar.activation(kTb[:, :, :], banks[:, 4:6, :], ACT.Copy).then_inc(k_ready, 1)
                for e in range(2):
                    nc.scalar.activation(kpar[:, :, :, e, :], by_seq(banks[:, 4:6, :]), ACT.Copy,
                                         scale=cst[:, C_PAR + e:C_PAR + e + 1]).then_inc(k_ready, 1)

            def v_out(g):
                act.wait_ge(v_mm, g + 1)
                for e in range(2):
                    r = slice(64 * e, 64 * e + 64)
                    nc.scalar.activation(vblk[r, :, :, e, :], v_psum[r], ACT.Copy).then_inc(v_ready, 1)

            def tanh(f, c, base=2):
                act.wait_ge(gate_mm, CH * f + c + 1)
                if c == 0 and later(f):
                    act.wait_ge(x3_steps, X3 * f)
                if c >= 2 or later(f):
                    act.wait_ge(h_lo, CH * f + c - 1)
                nc.scalar.activation(act_t[:, c % 2, :], banks[:, base, :], ACT.Tanh, scale=0.5)\
                    .then_inc(tanh_ready, 1)

            def hidden_hi(f, c):
                act.wait_ge(h_steps, 2 * CH * f + 2 * c + 2)
                if c >= 2 or later(f):
                    act.wait_ge(out_mm, CH * f + c - 1)
                nc.scalar.activation(hs[:, c % 2, 0, :], act_t[:, c % 2, :], ACT.Copy).then_inc(h_hi, 1)

            def exp(g, n, base=4):
                act.wait_ge(st_mm, 4 * g + n + 1)
                if n >= 2 or later(g):
                    act.wait_ge(o_mm, 2 * g + n // 2)
                b = 4 * (n % 2)
                nc.scalar.activation(pt[:, b:b + 4].rearrange("p b j q -> p (b j q)"),
                                     banks[:, base:base + 2, :].rearrange("p k n -> p (k n)"), ACT.Exp,
                                     scale=SCALE).then_inc(p_ready, 1)

            def o_split(g, h):
                act.wait_ge(o_steps, 4 * g + 2 * h + 2)
                nc.scalar.activation(os_[:, 0, h, :], work_c[:, 1, :], ACT.Copy).then_inc(o_hi, 1)

            def square(g):
                act.wait_ge(x2_steps, 2 * g + 2)
                act.wait_ge(o_lo, 2 * g + 2)
                nc.scalar.activation(work_c[:, :, :], x2[:, :, :], ACT.Square).then_inc(sq_ready, 1)

            def x2_split(g):
                for k in range(KD):
                    act.wait_ge(x2n_steps, 2 * KD * g + KD + k + 1)
                    nc.scalar.activation(x2s[:, 0, k], work_b[:, k, :], ACT.Copy).then_inc(x2s_hi, 1)

            def copy_x3(f):
                act.wait_ge(ft_mm, f + 1)
                if later(f):
                    act.wait_ge(out_stored, 16 * f)
                nc.scalar.activation(final[:, :, :].rearrange("p t n -> p (t n)"),
                                     banks[:, 2:4, :].rearrange("p k n -> p (k n)"), ACT.Copy)\
                    .then_inc(x3_tok, 1)

            def keep_x2(f):
                if later(f):
                    act.wait_ge(ft_mm, f)
                nc.scalar.activation(work_d[:, :, :], x2[:, :, :], ACT.Copy).then_inc(x2_kept, 1)

            def feed(f, c, base=2):
                tanh(f, c, base)
                hidden_hi(f, c)

            def head(g, norm2=True, ln=True):
                k_out(g)
                v_out(g)
                if ln:
                    copy_x3(g - 2)
                if norm2:
                    x2_split(g - 1)
                    keep_x2(g - 1)

            def main(g, fed=True, more=True):
                f = g - 1

                def fill(c):
                    if fed:
                        feed(f, c)
                    else:
                        for n in cut_in_slot(c):
                            cut_hi(n)
                for c in range(4):
                    fill(c)
                odd = 4 if fed else 2
                exp(g, 0)
                fill(4)
                exp(g, 1, odd)
                exp(g, 2)
                o_split(g, 0)
                fill(5)
                exp(g, 3, odd)
                o_split(g, 1)
                fill(6)
                if more:
                    xs_split(g + 1)
                if fed:
                    tanh(f, 7)
                square(g)
                if fed:
                    hidden_hi(f, 7)

            cut_hi(0)
            xs_split(0)
            cut_hi(1)
            act.wait_ge(setup_dve, SETUP_TANH)
            nc.scalar.activation(cvec[0:B], cvec[0:B], ACT.Tanh).then_inc(setup_act, 1)
            act.wait_ge(zeroed, 1)
            head(0, norm2=False, ln=False)
            main(0, fed=False)
            head(1, ln=False)
            act.wait_ge(shift_stored, 16)
            main(1)
            head(2)
            with act.Fori(2, GROUPS - 1) as i:
                main(i)
                head(i + 1)
            main(GROUPS - 1, more=False)
            copy_x3(GROUPS - 2)
            x2_split(GROUPS - 1)
            keep_x2(GROUPS - 1)
            for c in range(CH):
                feed(GROUPS - 1, c, 2 + 2 * (c % 2))

        @block.vector
        def _(dve):
            V = nc.vector

            def rsqrt(steps, n, v, y, t):
                V.tensor_scalar(y.bitcast(I32), v.bitcast(I32), -0.5, RSQRT_MAGIC, ALU.mult, ALU.add)\
                    .then_inc(steps, 1)
                dve.wait_ge(steps, n + 1)
                for r in range(NEWTON):
                    V.tensor_tensor(t, y, y, ALU.mult).then_inc(steps, 1)
                    dve.wait_ge(steps, n + 3 * r + 2)
                    V.scalar_tensor_tensor(out=t, in0=t, scalar=-0.5, in1=v, op0=ALU.mult, op1=ALU.mult)\
                        .then_inc(steps, 1)
                    dve.wait_ge(steps, n + 3 * r + 3)
                    V.scalar_tensor_tensor(out=y, in0=t, scalar=1.5, in1=y, op0=ALU.add, op1=ALU.mult)\
                        .then_inc(steps, 1)
                    dve.wait_ge(steps, n + 3 * r + 4)

            def setup_tables():
                dve.wait_ge(ld_tables, LD_TABLE)
                for e in range(2):
                    V.tensor_copy(identb[64 * e:64 * e + 64, :], ident[64 * e:64 * e + 64, 64 * e:64 * e + 64])\
                        .then_inc(identb_ready, 1)
                dve.wait_ge(tables_mm, 1)
                n = len(TABLES) * KD * B
                V.tensor_copy(tabs[:, :, :, :].rearrange("p t k b -> p (t k b)"),
                              banks[:, 0:2, :].rearrange("p k n -> p (k n)")[:, 0:n]).then_inc(tables_ready, 1)

            def setup_shift():
                dve.wait_ge(ld_lin, LD_SHIFT)
                dve.wait_ge(shift_mm, 1)
                V.tensor_tensor(cvec[0:B], banks[0:B, 2, 0:D], linb_b[0:B], ALU.add).then_inc(setup_dve, 1)
                V.tensor_tensor(w2[:, :], lnw_b, lnw_b, ALU.mult).then_inc(setup_dve, 1)
                dve.wait_ge(setup_act, 1)
                V.tensor_tensor(cvec[0:B], cvec[0:B], lnb_b[0:B], ALU.add).then_inc(setup_dve, 1)
                dve.wait_ge(setup_dve, 3)
                V.tensor_tensor(cvec[0:B], cvec[0:B], lnw_b[0:B], ALU.mult).then_inc(setup_dve, 1)
                dve.wait_ge(setup_dve, 4)
                V.tensor_tensor(cvec[0:B], cvec[0:B], lnb_b[0:B], ALU.add).then_inc(setup_dve, 1)

            def cut_lo(n):
                dve.wait_ge(stage_hi, n + 1)
                V.tensor_tensor(chunks[n][2], stage_view(n), chunks[n][1].bitcast(F32), ALU.subtract)\
                    .then_inc(stage_lo, 1)

            def stats_x(g):
                dve.wait_ge(ld_x, 16 * g + 16)
                for t in range(TT):
                    V.bn_stats(stat[:, 0, t, :], xtok[:, t, :]).then_inc(x_stats, 1)
                dve.wait_ge(x_stats, XS * g + TT)
                V.memset(nt1[:, 2, 0, :], 0.0)
                for t in range(TT):
                    V.bn_aggr(mv[:, 0, t, :], stat[:, 0, t, :]).then_inc(x_stats, 1)
                dve.wait_ge(x_stats, XS * g + 2 * TT)
                V.tensor_tensor(nt1[:, 2, 0, :], mv[:, 0, :, 0], mv[:, 0, :, 0], ALU.mult).then_inc(x_stats, 1)
                dve.wait_ge(x_stats, XS * g + 2 * TT + 1)
                V.scalar_tensor_tensor(out=nt1[:, 0, 0, :], in0=nt1[:, 2, 0, :], scalar=EPS_RMS,
                                       in1=mv[:, 0, :, 1], op0=ALU.add, op1=ALU.add).then_inc(x_stats, 1)

            def stats_x3(f, tile=lambda t: final[:, t, :]):
                for t in range(TT):
                    V.bn_stats(stat[:, 1, t, :], tile(t)).then_inc(ln_stats, 1)
                dve.wait_ge(ln_stats, LS * f + TT)
                V.memset(nt1[:, 2, 1, :], 0.0)
                for t in range(TT):
                    V.bn_aggr(mv[:, 1, t, :], stat[:, 1, t, :]).then_inc(ln_stats, 1)
                dve.wait_ge(ln_stats, LS * f + 2 * TT)
                V.tensor_scalar(nt1[:, 0, 1, :], mv[:, 1, :, 1], EPS_LN, None, ALU.add).then_inc(ln_stats, 1)

            def rsqrt_both(n):
                v, y, t = (nt1[:, i].rearrange("p a t -> p (a t)") for i in range(3))
                rsqrt(norm1_steps, RS * n, v, y, t)

            def scale_xn(g):
                dve.wait_ge(xt_mm, g + 1)
                V.tensor_tensor(by_seq(xn[:, :, :]), by_seq(banks[:, 4:6, :]), table(GA, g), ALU.mult)\
                    .then_inc(xn_gamma, 1)

            def q_out(g):
                dve.wait_ge(q_mm, g + 1)
                V.tensor_copy(qT[:, :, :], banks[:, 4:6, :]).then_inc(q_ready, 1)
                dve.wait_ge(q_ready, 3 * g + 1)
                for e in range(2):
                    V.tensor_scalar(qpar[:, :, :, e, :], by_seq(qT[:, :, :]),
                                    cst[:, C_PAR + e:C_PAR + e + 1], None, ALU.mult).then_inc(q_ready, 1)

            def max_over_keys(g, n):
                dve.wait_ge(s_mm, 4 * g + n + 1)
                base = 6 - 2 * (n % 2)
                V.tensor_reduce(smax[:, 16 * n:16 * n + 16],
                                banks[:, base:base + 2, :].rearrange("p k (r c) -> p (k r) c", c=L),
                                AX.X, ALU.max).then_inc(max_ready, 1)

            def negate_max(g):
                dve.wait_ge(mt_mm, g + 1)
                V.tensor_tensor(negmax[:, :, :], max_t.unsqueeze(1).to_broadcast([P, J, L]),
                                cst[:, C_NEG:C_NEG + J].unsqueeze(2).to_broadcast([P, J, L]), ALU.mult)\
                    .then_inc(negmax_ready, 1)

            def normalise(g, h):
                dve.wait_ge(den_mm, 2 * g + h + 1)
                V.reciprocal(work_c[:, 0, :], banks[:, 7, :]).then_inc(o_steps, 1)
                dve.wait_ge(o_steps, 4 * g + 2 * h + 1)
                dve.wait_ge(o_mm, 2 * g + h + 1)
                if h:
                    dve.wait_ge(o_hi, 2 * g + 1)
                    dve.wait_ge(o_lo, 2 * g + 1)
                V.tensor_tensor(work_c[:, 1, :], banks[:, 6, :], work_c[:, 0, :], ALU.mult).then_inc(o_steps, 1)

            def residual1(g):
                dve.wait_ge(op_mm, g + 1)
                dve.wait_ge(ld_res, 16 * g + 16)
                V.tensor_tensor(by_seq(work_b[:, :, :]), by_seq(banks[:, 6:8, :]), table(AA, g), ALU.mult)\
                    .then_inc(x2_steps, 1)
                dve.wait_ge(x2_steps, 2 * g + 1)
                V.tensor_tensor(x2[:, :, :], work_b[:, :, :], xres[:, :, :], ALU.add).then_inc(x2_steps, 1)

            def norm2(g):
                v, y, t = (nt2[:, i, :] for i in range(3))
                dve.wait_ge(ss_mm, g + 1)
                V.tensor_scalar(v, banks[:, 7, 0:P], 1.0 / D, EPS_RMS, ALU.mult, ALU.add).then_inc(norm2_steps, 1)
                dve.wait_ge(norm2_steps, N2 * g + 1)
                rsqrt(norm2_steps, N2 * g + 1, v, y, t)

            def scale_x2(g):
                dve.wait_ge(x2_gamma, g + 1)
                dve.wait_ge(rb_mm, g + 1)
                for k in range(KD):
                    V.tensor_tensor(work_b[:, k, :], work_b[:, k, :], banks[:, 1, :], ALU.mult)\
                        .then_inc(x2n_steps, 1)
                for k in range(KD):
                    dve.wait_ge(x2n_steps, 2 * KD * g + k + 1)
                    V.tensor_tensor(by_token(work_b[:, k, :]), by_token(work_b[:, k, :]), table(BF, g, k), ALU.add)\
                        .then_inc(x2n_steps, 1)

            def feed(f, c, base=2):
                a = act_t[:, c % 2, :]
                dve.wait_ge(tanh_ready, CH * f + c + 1)
                V.scalar_tensor_tensor(out=a, in0=a, scalar=1.0, in1=banks[:, base, :], op0=ALU.add,
                                       op1=ALU.mult).then_inc(h_steps, 1)
                dve.wait_ge(h_steps, 2 * CH * f + 2 * c + 1)
                dve.wait_ge(hidden_mm, CH * f + c + 1)
                V.scalar_tensor_tensor(out=a, in0=a, scalar=0.5, in1=banks[:, base + 1, :], op0=ALU.mult,
                                       op1=ALU.mult).then_inc(h_steps, 1)

            def residual2(f):
                dve.wait_ge(out_mm, CH * f + CH)
                dve.wait_ge(h_lo, CH * f + CH)
                for m in range(KD):
                    V.scalar_tensor_tensor(
                        out=by_token(act_t[:, m, :]), in0=by_token(banks[:, m, :]), scalar=outb[:, m:m + 1],
                        in1=table(AF, f, m), op0=ALU.add, op1=ALU.mult).then_inc(x3_steps, 1)
                dve.wait_ge(x2_kept, f + 1)
                for m in range(KD):
                    dve.wait_ge(x3_steps, X3 * f + m + 1)
                    V.tensor_tensor(work_d[:, m, :], work_d[:, m, :], act_t[:, m, :], ALU.add).then_inc(x3_steps, 1)

            def finish(f, tile=lambda t: final[:, t, :]):
                for t in range(TT):
                    V.scalar_tensor_tensor(out=final[:, t, :], in0=tile(t), scalar=mv[:, 1, t, 0:1],
                                           in1=w2[:, :], op0=ALU.subtract, op1=ALU.mult).then_inc(final_steps, 1)
                dve.wait_ge(ld_shift, 32 * f + 32)
                for t in range(TT):
                    dve.wait_ge(final_steps, FS * f + t + 1)
                    V.scalar_tensor_tensor(out=final[:, t, :], in0=final[:, t, :], scalar=nt1[:, 1, 1, t:t + 1],
                                           in1=shift[:, t, :], op0=ALU.mult, op1=ALU.add).then_inc(final_steps, 1)

            def head(g, norm2_=True, ln=True):
                if norm2_:
                    norm2(g - 1)
                if ln:
                    residual2(g - 2)
                if norm2_:
                    scale_x2(g - 1)
                q_out(g)

            def main(g, fed=True, more=True, ln=True):
                f = g - 1

                def fill(c):
                    if fed:
                        feed(f, c)
                    else:
                        for n in cut_in_slot(c):
                            cut_lo(n)
                fill(0)
                max_over_keys(g, 0)
                max_over_keys(g, 1)
                fill(1)
                max_over_keys(g, 2)
                max_over_keys(g, 3)
                fill(2)
                negate_max(g)
                if more:
                    stats_x(g + 1)
                fill(3)
                if ln:
                    dve.wait_ge(x3_tok, g - 1)
                    stats_x3(g - 2)
                if more:
                    dve.wait_ge(x_stats, XS * (g + 2))
                if ln:
                    dve.wait_ge(ln_stats, LS * (g - 1))
                rsqrt_both(g + 1)
                fill(4)
                if ln:
                    finish(g - 2)
                normalise(g, 0)
                fill(5)
                normalise(g, 1)
                fill(6)
                if more:
                    scale_xn(g + 1)
                residual1(g)
                fill(7)

            V.memset(nt1[:, :, :, :], 1.0).then_inc(nt1_set, 1)
            dve.wait_ge(nt1_set, 1)
            stats_x(0)
            dve.wait_ge(x_stats, XS)
            rsqrt_both(0)
            setup_tables()
            dve.wait_ge(tables_ready, 1)
            scale_xn(0)
            cut_lo(0)
            cut_lo(1)
            setup_shift()
            head(0, norm2_=False, ln=False)
            main(0, fed=False, ln=False)
            head(1, ln=False)
            main(1, ln=False)
            head(2)
            with dve.Fori(2, GROUPS - 1) as i:
                main(i)
                head(i + 1)
            main(GROUPS - 1, more=False)
            norm2(GROUPS - 1)
            residual2(GROUPS - 2)
            scale_x2(GROUPS - 1)
            for c in range(CH):
                feed(GROUPS - 1, c, 2 + 2 * (c % 2))
                if c == 1:
                    dve.wait_ge(x3_tok, GROUPS - 1)
                    stats_x3(GROUPS - 2)
                    dve.wait_ge(ln_stats, LS * (GROUPS - 1))
                    rsqrt_both(GROUPS + 1)
                if c == 3:
                    finish(GROUPS - 2)
            residual2(GROUPS - 1)

            def in_banks(t):
                return banks[:, 2 + t // 2, 256 * (t % 2):256 * (t % 2) + D]

            dve.wait_ge(ft_mm, GROUPS)
            stats_x3(GROUPS - 1, in_banks)
            dve.wait_ge(ln_stats, LS * GROUPS)
            rsqrt_both(GROUPS + 2)
            dve.wait_ge(out_stored, 16 * (GROUPS - 1))
            finish(GROUPS - 1, in_banks)

        @block.gpsimd
        def _(pool):
            tt = nc.gpsimd.tensor_tensor

            def scale_x(g):
                pool.wait_ge(norm1_steps, RS * g + RS)
                tt(xtok[:, :, :], xtok[:, :, :], nt1[:, 1, 0, :].unsqueeze(2).to_broadcast([P, TT, D]),
                   ALU.mult).then_inc(xs_scaled, 1)

            def shift_xn(g):
                pool.wait_ge(xn_gamma, g + 1)
                tt(by_seq(xn[:, :, :]), by_seq(xn[:, :, :]), table(BA, g), ALU.add).then_inc(xn_beta, 1)

            def xs_split(g):
                pool.wait_ge(xs_hi, g + 1)
                tt(xs[:, 1], xn[:, :, :], xs[:, 0].bitcast(F32), ALU.subtract).then_inc(xs_lo, 1)

            def o_split(g, h):
                pool.wait_ge(o_hi, 2 * g + h + 1)
                tt(os_[:, 1, h, :], work_c[:, 1, :], os_[:, 0, h, :].bitcast(F32), ALU.subtract).then_inc(o_lo, 1)

            def x2_by_gamma(g):
                pool.wait_ge(x2_steps, 2 * g + 2)
                tt(by_seq(work_b[:, :, :]), by_seq(x2[:, :, :]), table(GF, g), ALU.mult).then_inc(x2_gamma, 1)

            def x2_split(g):
                for k in range(KD):
                    pool.wait_ge(x2s_hi, KD * g + k + 1)
                    tt(x2s[:, 1, k], work_b[:, k, :], x2s[:, 0, k].bitcast(F32), ALU.subtract).then_inc(x2s_lo, 1)

            def hidden_lo(f, c):
                pool.wait_ge(h_hi, CH * f + c + 1)
                tt(hs[:, c % 2, 1, :], act_t[:, c % 2, :], hs[:, c % 2, 0, :].bitcast(F32), ALU.subtract)\
                    .then_inc(h_lo, 1)

            def main(g, fed=True, more=True):
                f = g - 1

                def fill(c):
                    if fed:
                        hidden_lo(f, c)
                for c in range(5):
                    fill(c)
                    if more and c == 3:
                        scale_x(g + 1)
                o_split(g, 0)
                fill(5)
                o_split(g, 1)
                fill(6)
                if more:
                    shift_xn(g + 1)
                    xs_split(g + 1)
                x2_by_gamma(g)
                fill(7)

            nc.gpsimd.memset(vblk[:, :, :, :, :], 0.0).then_inc(zeroed, 1)
            nc.gpsimd.memset(kpair[:, :, :, :], 0.0).then_inc(zeroed, 1)
            scale_x(0)
            pool.wait_ge(tables_ready, 1)
            shift_xn(0)
            xs_split(0)
            nc.gpsimd.memset(qpair[:, :, :, :], 0.0).then_inc(zeroed, 1)
            nc.gpsimd.tensor_copy(sel[:, :, :].rearrange("p c (e k) -> p (c e) k", e=2),
                                  cst[:, C_SEL:C_SEL + 2 * G * SEQ].unsqueeze(2).to_broadcast([P, 2 * G * SEQ, L]))\
                .then_inc(selectors_ready, 1)
            nc.gpsimd.tensor_copy(row[:, :, :], cst[:, C_ROW:C_ROW + TT].unsqueeze(2).to_broadcast([P, TT, P]))\
                .then_inc(selectors_ready, 1)
            main(0, fed=False)
            x2_split(0)
            main(1)
            x2_split(1)
            with pool.Fori(2, GROUPS - 1) as i:
                main(i)
                x2_split(i)
            main(GROUPS - 1, more=False)
            x2_split(GROUPS - 1)
            for c in range(CH):
                hidden_lo(GROUPS - 1, c)


def kernel(x, cond_256, L1_cond_weight, L1_cond_bias, L1_cond_lin_w, L1_cond_lin_b, **w):
    import concourse.bacc as bacc
    from concourse.bass_utils import run_bass_kernel_spmd

    def layer0(name):
        return np.asarray(w["L0_cond_" + name])

    x = np.asarray(x)
    arrays = dict(
        x=x,
        xT=x.reshape(B * L, D).T,
        condT=np.asarray(cond_256).T,
        tabT=np.stack([layer0(t + "_w").T for t in TABLES], axis=1),
        linT=np.asarray(L1_cond_lin_w).T,
        linb=np.asarray(L1_cond_lin_b).reshape(1, D),
        lnw=np.asarray(L1_cond_weight).reshape(1, D),
        lnb=np.asarray(L1_cond_bias).reshape(1, D),
        wqkT=np.concatenate([layer0("W_q").T, layer0("W_k").T], axis=1),
        wvT=layer0("W_v").T,
        woT=layer0("W_o").T,
        ghT=np.concatenate([layer0("gate_w").T, layer0("hidden_w").T], axis=1),
        outT=layer0("out_w").T,
        outb=layer0("out_b").reshape(KD, P).T,
        consts=shape_constants(),
    )
    arrays = {k + "_in": np.ascontiguousarray(a) for k, a in arrays.items()}
    nc = bacc.Bacc("TRN2", target_bir_lowering=False, num_devices=1)
    args = [nc.dram_tensor(k, a.shape, mybir.dt.from_np(a.dtype), kind="ExternalInput").ap()
            for k, a in arrays.items()]
    args.append(nc.dram_tensor("y", (B, L, D), F32, kind="ExternalOutput").ap())
    build(nc, *args)
    r = run_bass_kernel_spmd(nc, [arrays], core_ids=[0])
    return r.results[0]["y"]
```

```python
from contextlib import ExitStack

import numpy as np

import concourse.bass as bass
from concourse import mybir

F32, F32R, BF16, I32 = mybir.dt.float32, mybir.dt.float32r, mybir.dt.bfloat16, mybir.dt.int32
ALU, ACT, AX = mybir.AluOpType, mybir.ActivationFunctionType, mybir.AxisListType

P = 128
B, L, D = 64, 64, 256
HEADS, DH = 16, 16
DT = 64
HID = 4 * D
KD = D // P
SEQ = 8
TOK = SEQ * L
GROUPS = B // SEQ
TT = TOK // P
G = 2
J = 4
CH = HID // P
SCALE = (HEADS / D) ** 0.5
EPS_RMS, EPS_LN = 1e-6, 1e-5
NEWTON = 3
LD_TABLE = 16 * 3
LD_SHIFT = 16 * 5
SETUP_TANH, SETUP_SHIFT = 1, 5
WARM_LOADS, WARM_TABLES, WARM_WEIGHTS, WARM_OUTPUT, WARM_NORM = 3, 2, 2, 6, 6
ZEROED = 3
RSQRT_MAGIC = float(0x5F3759DF)
TABLES = ("attn_gamma", "attn_beta", "attn_alpha", "ffn_gamma", "ffn_beta", "ffn_alpha")
GA, BA, AA, GF, BF, AF = range(6)
FIRST_TABLES, OTHER_TABLES = (GA, BA), (AA, GF, BF, AF)
TABLE_BANK = {FIRST_TABLES: 3, OTHER_TABLES: 0}

C_ID, C_PAR, C_NEG, C_BLK, C_ONE, C_ROW, C_SEL = 0, 128, 130, 134, 166, 198, 202
C_END = C_SEL + G * SEQ * 2


def shape_constants():
    c = np.zeros((P, C_END), np.float32)
    p = np.arange(P)
    c[p, C_ID + p] = 1
    c[p, C_PAR + (p // DH) % 2] = 1
    c[p, C_NEG + p % J] = -1
    for e in range(2):
        c[64 * e:64 * e + 64, C_BLK + DH * e:C_BLK + DH * e + DH] = 1
    c[:, C_ONE:C_ONE + 32] = 1
    for t in range(TT):
        c[32 * t, C_ROW + t] = 1
    for r in range(P):
        c[r, C_SEL + 2 * ((r % 64) // J) + r // 64] = 1
    return c


def build(nc, x, xT, condT, tabT, linT, linb, lnw, lnb, wqkT, wvT, woT, ghT, outT, outb_dram,
          consts, out):
    with ExitStack() as ctx:
        def sb(name, shape, dt=F32):
            return ctx.enter_context(nc.sbuf_tensor(name, shape, dt))

        def sem(name):
            return ctx.enter_context(nc.semaphore(name))

        cst = sb("cst", [P, C_END])
        sel = sb("sel", [P, G * SEQ, P], BF16)
        row = sb("row", [P, TT, P])
        identb = sb("identb", [P, 64], BF16)
        wqk = sb("wqk", [P, 2, KD, 2 * D], F32R)
        wv = sb("wv", [P, 2, KD, D], F32R)
        wo = sb("wo", [P, 2, KD, D], F32R)
        gh = sb("gh", [P, 2, KD, 2 * HID], F32R)
        wout = sb("wout", [P, 2, CH, D], F32R)
        outb = sb("outb", [P, KD])
        tabs = sb("tabs", [P, len(TABLES), KD, B])
        w2 = sb("w2", [P, D])
        xtok = sb("xtok", [P, TT, D])
        xres = sb("xres", [P, KD, TOK])
        xn = sb("xn", [P, KD, TOK])
        xs = sb("xs", [P, 2, KD, TOK], F32R)
        qT = sb("qT", [P, G, TOK])
        kTb = sb("kTb", [P, G, TOK], BF16)
        qpar = sb("qpar", [P, G, SEQ, 2, L], BF16)
        kpar = sb("kpar", [P, G, SEQ, 2, L])
        qpair = sb("qpair", [P, G, J, TOK])
        kpair = sb("kpair", [P, G, J, TOK], BF16)
        vblk = sb("vblk", [P, SEQ, G * J, 2, DH])
        smax = sb("smax", [P, G * SEQ * J], BF16)
        negmax = sb("negmax", [P, J, L], BF16)
        pt = sb("pt", [P, SEQ, J, L])
        work_b = sb("work_b", [P, KD, TOK])
        work_c = sb("work_c", [P, 2, TOK])
        work_d = sb("work_d", [P, KD, TOK])
        os_ = sb("os", [P, 2, G, TOK], F32R)
        x2 = sb("x2", [P, KD, TOK])
        x2s = sb("x2s", [P, 2, KD, TOK], F32R)
        act_t = sb("act_t", [P, 2, TOK])
        hs = sb("hs", [P, 2, 2, TOK], F32R)
        final = sb("final", [P, TT, D])
        shift = sb("shift", [P, TT, D])
        stat = sb("stat", [P, 2, TT, 6])
        mv = sb("mv", [P, 2, TT, 2])
        nt1 = sb("nt1", [P, 3, 2, TT])
        nt2 = sb("nt2", [P, 3, P])
        banks = ctx.enter_context(nc.psum_tensor("banks", [P, 8, 512], F32))
        shift_dram = nc.dram_tensor("shift_dram", [B, D], F32, kind="Internal").ap()

        ident = cst[:, C_ID:C_ID + P]
        setup_area = pt[0:DT].rearrange("p b j q -> p (b j q)")
        n_tab = len(TABLES) * D
        tabw = setup_area[:, 0:n_tab].rearrange("p (t n) -> p t n", n=D)
        linw = setup_area[:, n_tab:n_tab + D]
        cond = setup_area[:, n_tab + D:n_tab + D + B]
        lnw_b, lnb_b, linb_b = final[:, 0, :], final[:, 1, :], final[:, 2, :]
        cvec = final[:, 3, :]
        v_kept, v_swapped = (a[:, :, :].rearrange("p k n -> p (k n)") for a in (xn, work_c))
        max_t = banks[:, 6, :].bitcast(BF16)[:, 0:L]


        ld_tables, ld_lin, ld_x, ld_res, ld_shift = map(
            sem, ("ld_tables", "ld_lin", "ld_x", "ld_res", "ld_shift"))
        ld_stage = (sem("ld_stage0"), sem("ld_stage1"))
        kpair_moved, qpair_moved, out_stored, shift_stored = map(
            sem, ("kpair_moved", "qpair_moved", "out_stored", "shift_stored"))
        zeroed, selectors_ready = sem("zeroed"), sem("selectors_ready")
        tables_mm, shift_mm, tables_ready, identb_ready, setup_dve, setup_act = map(
            sem, ("tables_mm", "shift_mm", "tables_ready", "identb_ready", "setup_dve", "setup_act"))
        stage_hi, stage_lo = sem("stage_hi"), sem("stage_lo")
        k_mm, q_mm, v_mm, s_mm, mt_mm, st_mm, den_mm, o_mm, xt_mm, op_mm, ss_mm, rb_mm, gate_mm, hidden_mm, out_mm, ft_mm = map(
            sem, ("k_mm", "q_mm", "v_mm", "s_mm", "mt_mm", "st_mm", "den_mm", "o_mm", "xt_mm", "op_mm", "ss_mm",
                  "rb_mm", "gate_mm", "hidden_mm", "out_mm", "ft_mm"))
        k_ready, q_ready, v_out, v_moved, v_ready, max_ready, negmax_ready, p_ready = map(
            sem, ("k_ready", "q_ready", "v_out", "v_moved", "v_ready", "max_ready", "negmax_ready", "p_ready"))
        nt1_set, x_stats, norm1_steps, xs_scaled, xn_gamma, xn_beta, xs_hi, xs_lo = map(
            sem, ("nt1_set", "x_stats", "norm1_steps", "xs_scaled", "xn_gamma", "xn_beta", "xs_hi", "xs_lo"))
        o_steps, o_hi, o_lo, x2_steps, sq_ready, x2_gamma = map(
            sem, ("o_steps", "o_hi", "o_lo", "x2_steps", "sq_ready", "x2_gamma"))
        norm2_steps, x2n_steps, x2s_hi, x2s_lo = map(
            sem, ("norm2_steps", "x2n_steps", "x2s_hi", "x2s_lo"))
        tanh_ready, h_steps, h_hi, h_lo = map(sem, ("tanh_ready", "h_steps", "h_hi", "h_lo"))
        x2_kept, x3_steps, x3_tok, ln_stats, final_steps = map(
            sem, ("x2_kept", "x3_steps", "x3_tok", "ln_stats", "final_steps"))


        stage = (work_b, work_d)

        def ktiles(a):
            return a.rearrange("(k p) n -> p k n", p=P)

        chunks = [(ktiles(w), parts[:, 0], parts[:, 1]) for w, parts in ((wqkT, wqk), (wvT, wv), (woT, wo))]
        EARLY = len(chunks)
        for k in range(KD):
            for h in range(2):
                cols = slice(HID * h, HID * h + HID)
                chunks.append((ktiles(ghT)[:, k, cols], gh[:, 0, k, cols], gh[:, 1, k, cols]))
        for h in range(2):
            cs = slice(CH // 2 * h, CH // 2 * h + CH // 2)
            chunks.append((ktiles(outT)[:, cs], wout[:, 0, cs], wout[:, 1, cs]))

        def stage_view(n):
            flat = stage[n % 2][:, :, :].rearrange("p a n -> p (a n)")
            shape = chunks[n][1].shape
            flat = flat[:, 0:int(np.prod(shape[1:]))]
            return flat if len(shape) == 2 else flat.rearrange("p (a n) -> p a n", a=shape[1])

        def cut_in_slot(c):
            return range(EARLY + 2 * (c - 2), EARLY + 2 * (c - 1)) if 3 <= c <= 4 else ()

        def later(g):
            return not isinstance(g, int) or g > 0

        def bank_of_s(g, n):
            return 6 - 2 * (n % 2) if later(g) else 4 + 2 * (n % 2)

        def table(t, g, m=None):
            if m is not None:
                return tabs[:, t, m, bass.ds(g * SEQ, SEQ)].unsqueeze(2).to_broadcast([P, SEQ, L])
            return tabs[:, t, :, bass.ds(g * SEQ, SEQ)].unsqueeze(3).to_broadcast([P, KD, SEQ, L])

        def by_seq(ap):
            return ap.rearrange("p k (b t) -> p k b t", b=SEQ)

        def by_token(ap):
            return ap.rearrange("p (b t) -> p b t", b=SEQ)

        x_v = x.rearrange("(g c b) t f -> g (b t) c f", g=GROUPS, c=TT)
        out_v = out.rearrange("(g c b) t f -> g (b t) c f", g=GROUPS, c=TT)
        xT_v = xT.rearrange("(k p) (g n) -> g p k n", p=P, g=GROUPS)
        shift_v = shift_dram.rearrange("(g c b) f -> g b c f", g=GROUPS, c=TT)
        passes = [(k, a, b) for a, b in ((0, 0), (1, 0), (0, 1)) for k in range(KD)]


        RS = 1 + 3 * NEWTON
        N2 = 1 + RS
        XS, LS = 2 * TT + 2, 2 * TT + 1
        X3, FS = 2 * KD, 2 * TT
        block = ctx.enter_context(nc.Block())

        @block.sync
        def _(sp):
            def load_stage(n):
                if n >= 2:
                    sp.wait_ge(stage_hi, n - 1)
                    sp.wait_ge(stage_lo, n - 1)
                sp.dma_start(stage_view(n), chunks[n][0]).then_inc(ld_stage[n % 2], 16)

            def load_x(g):
                if later(g):
                    sp.wait_ge(xt_mm, g)
                sp.dma_start(xtok[:, :, :], x_v[g]).then_inc(ld_x, 16)

            def load_res(g):
                if later(g):
                    sp.wait_ge(x2_steps, 2 * g)
                sp.dma_start(xres[:, :, :], xT_v[g]).then_inc(ld_res, 16)

            def load_shift(f):
                if later(f):
                    sp.wait_ge(final_steps, FS * f)
                for b in range(2):
                    sp.dma_start(shift[64 * b:64 * b + 64, :, :],
                                 shift_v[f][b:b + 1].to_broadcast([L, TT, D])).then_inc(ld_shift, 16)

            def move_k(g):
                sp.wait_ge(k_ready, 3 * g + 1)
                for j in range(J):
                    r = slice(32 * j, 32 * j + 32)
                    sp.dma_start(kpair[r, :, j, :], kTb[r, :, :]).then_inc(kpair_moved, 16)

            def move_q(g):
                sp.wait_ge(q_ready, 6 * g + 2)
                for j in range(J):
                    r = slice(32 * j, 32 * j + 32)
                    sp.dma_start(qpair[r, :, j, :], qT[r, :, :]).then_inc(qpair_moved, 16)

            def move_v(g):
                sp.wait_ge(v_out, g + 1)
                if later(g):
                    sp.wait_ge(ss_mm, g)
                for e in range(2):
                    sp.dma_start(v_swapped[64 * e:64 * e + 64], v_kept[64 - 64 * e:128 - 64 * e])\
                        .then_inc(v_moved, 16)

            def store(f):
                sp.wait_ge(final_steps, FS * f + FS)
                sp.dma_start(out_v[f], final[:, :, :]).then_inc(out_stored, 16)

            load_x(0)
            sp.dma_start(tabw, tabT).then_inc(ld_tables, 16)
            sp.dma_start(cond, condT).then_inc(ld_tables, 16)
            sp.dma_start(cst[:, :], consts).then_inc(ld_tables, 16)
            load_stage(0)
            load_stage(1)
            sp.dma_start(linw, linT).then_inc(ld_lin, 16)
            for dst, src in ((lnw_b, lnw), (lnb_b, lnb), (linb_b, linb)):
                sp.dma_start(dst, src.to_broadcast([P, D])).then_inc(ld_lin, 16)
            sp.dma_start(outb[:, :], outb_dram).then_inc(ld_lin, 16)
            for n in range(2, EARLY + 1):
                load_stage(n)
            sp.wait_ge(zeroed, ZEROED)
            move_k(0)
            move_q(0)
            load_stage(EARLY + 1)
            move_v(0)
            load_x(1)
            load_stage(EARLY + 2)
            load_stage(EARLY + 3)
            load_res(0)
            sp.wait_ge(setup_dve, SETUP_SHIFT)
            sp.dma_start(shift_dram, cvec[0:B]).then_inc(shift_stored, 16)
            for n in range(EARLY + 4, len(chunks)):
                load_stage(n)
            move_k(1)
            move_v(1)
            move_q(1)

            def step(i, first=False):
                load_x(i + 1)
                load_res(i)
                if first:
                    sp.wait_ge(shift_stored, 16)
                    load_shift(0)
                else:
                    store(i - 2)
                    load_shift(i - 1)
                move_k(i + 1)
                move_v(i + 1)
                move_q(i + 1)

            step(1, first=True)
            with sp.Fori(2, GROUPS - 1) as i:
                step(i)
            load_res(GROUPS - 1)
            store(GROUPS - 3)
            load_shift(GROUPS - 2)
            store(GROUPS - 2)
            load_shift(GROUPS - 1)
            for t in range(TT):
                sp.wait_ge(final_steps, FS * (GROUPS - 1) + TT + t + 1)
                sp.dma_start(out_v[GROUPS - 1][:, t], final[:, t, :]).then_inc(out_stored, 16)
            sp.wait_ge(out_stored, 16 * (GROUPS - 1 + TT))

        @block.tensor
        def _(pe):
            mm = nc.tensor.matmul

            def warm_up(operand, n, bank=1):
                for _ in range(n):
                    mm(banks[:, bank, :], operand[:, 0:P], operand, start=True, stop=True)

            def setup_tables(names):
                pe.wait_ge(ld_tables, LD_TABLE)
                for i, t in enumerate(names):
                    for k in range(KD):
                        c = (i * KD + k) * B
                        last = mm(banks[:, TABLE_BANK[names], c:c + B], tabw[:, t, P * k:P * k + P], cond,
                                  start=True, stop=True)
                last.then_inc(tables_mm, 1)

            def setup_shift():
                pe.wait_ge(ld_lin, LD_SHIFT)
                mm(banks[0:B, 2, 0:D], cond, linw, start=True, stop=True).then_inc(shift_mm, 1)

            def transpose_x(g):
                pe.wait_ge(xs_scaled, g + 2 if later(g) else 1)
                if later(g):
                    pe.wait_ge(p_ready, 4 * g)
                steps = [(t, k) for t in range(TT) for k in range(KD)]
                for n, (t, k) in enumerate(steps):
                    if not later(g) and n == len(steps) // 2:
                        pe.wait_ge(xs_scaled, 2)
                    if isinstance(g, int) and g == 1 and n == len(steps) // 2:
                        pe.wait_ge(o_steps, 3)
                    last = nc.tensor.transpose(banks[:, 4 + k, P * t:P * t + P],
                                               xtok[:, t, P * k:P * k + P], ident)
                last.then_inc(xt_mm, 1)

            def project_qk(g, which, base, done):
                for m in range(G):
                    c = D * which + P * m
                    for n, (k, a, b) in enumerate(passes):
                        if b and m == 0:
                            pe.wait_ge(xs_lo, g + 1)
                        last = mm(banks[:, base + m, :], wqk[:, a, k, c:c + P], xs[:, b, k, :],
                                  start=(n == 0), stop=(n == 5))
                last.then_inc(done, 1)

            def k_proj(g):
                pe.wait_ge(xs_hi, g + 1)
                project_qk(g, 1, 4, k_mm)

            def q_proj(g):
                if later(g):
                    pe.wait_ge(k_ready, 3 * g + 3)
                    project_qk(g, 0, 4, q_mm)
                else:
                    pe.wait_ge(tables_ready, 2)
                    project_qk(g, 0, 0, q_mm)

            def v_proj(g):
                if later(g):
                    pe.wait_ge(x2_steps, 2 * g)
                    pe.wait_ge(norm2_steps, N2 * (g - 1) + 1)
                else:
                    pe.wait_ge(stage_lo, 2)
                for t in range(TT):
                    for n, (k, a, b) in enumerate(passes):
                        last = mm(banks[:, 6 + t // 2, D * (t % 2):D * (t % 2) + D],
                                  xs[:, a, k, P * t:P * t + P], wv[:, b, k, :], start=(n == 0), stop=(n == 5))
                last.then_inc(v_mm, 1)

            def scores_for_max(g, n):
                if not later(g):
                    if n == 0:
                        pe.wait_ge(k_ready, 3)
                        pe.wait_ge(kpair_moved, 64)
                        pe.wait_ge(q_ready, 4)
                    if n == 1:
                        pe.wait_ge(v_out, 1)
                    if n >= 2:
                        pe.wait_ge(max_ready, n - 1)
                elif n == 0:
                    pe.wait_ge(v_out, g + 1)
                    pe.wait_ge(kpair_moved, 64 * g + 64)
                    pe.wait_ge(q_ready, 6 * g + 4)
                else:
                    pe.wait_ge(max_ready, 4 * g + n - 1)
                if n == 2:
                    pe.wait_ge(q_ready, 6 * g + 6)
                h, base = n // 2, bank_of_s(g, n)
                for i in range(4):
                    b = 4 * (n % 2) + i
                    last = mm(banks[:, base + i // 2, 256 * (i % 2):256 * (i % 2) + 256], qpar[:, h, b],
                              kpair[:, h, :, L * b:L * b + L], start=True, stop=True)
                last.then_inc(s_mm, 1)

            def transpose_max(g):
                for e in range(2):
                    r = slice(64 * e, 64 * e + 64)
                    last = nc.tensor.transpose(max_t[r, :], smax[r, :], identb[r, :])
                last.then_inc(mt_mm, 1)

            def scores(g, n, alternate=False):
                h, base = n // 2, 2 if alternate and n % 2 else 4
                if n == 0:
                    if not later(g):
                        pe.wait_ge(selectors_ready, 1)
                    pe.wait_ge(negmax_ready, g + 1)
                    pe.wait_ge(qpair_moved, 64 * g + 64)
                elif not alternate:
                    pe.wait_ge(p_ready, 4 * g + n)
                elif n >= 2:
                    pe.wait_ge(p_ready, 4 * g + n - 1)
                for i in range(4):
                    b = 4 * (n % 2) + i
                    dst = banks[:, base + i // 2, 256 * (i % 2):256 * (i % 2) + 256]
                    mm(dst, kpar[:, h, b], qpair[:, h, :, L * b:L * b + L], start=True, stop=False)
                    last = mm(dst, sel[:, SEQ * h + b], negmax[:, :, :], start=False, stop=True)
                last.then_inc(st_mm, 1)

            def attend(g, h):
                pe.wait_ge(p_ready, 4 * g + 2 * h + 2)
                if h:
                    pe.wait_ge(o_steps, 4 * g + 2)
                else:
                    pe.wait_ge(v_ready, 4 * g + 4)
                for j in range(J):
                    last = mm(banks[32 * j:32 * j + 32, 7, :], cst[:, C_BLK:C_BLK + 32], pt[:, :, j, :],
                              start=True, stop=True)
                last.then_inc(den_mm, 1)
                for b in range(SEQ):
                    for j in range(J):
                        last = mm(banks[32 * j:32 * j + 32, 6, L * b:L * b + L], vblk[:, b, J * h + j],
                                  pt[:, b, j, :], start=True, stop=True)
                last.then_inc(o_mm, 1)

            def o_proj(g):
                pe.wait_ge(o_hi, 2 * g + 2)
                pe.wait_ge(o_lo, 2 * g + 2)
                for m in range(KD):
                    for n, (k, a, b) in enumerate(passes):
                        last = mm(banks[:, 6 + m, :], wo[:, a, k, P * m:P * m + P], os_[:, b, k, :],
                                  start=(n == 0), stop=(n == 5))
                last.then_inc(op_mm, 1)

            def square_sums(g):
                pe.wait_ge(sq_ready, g + 1)
                for t in range(TT):
                    for k in range(KD):
                        last = mm(banks[32 * t:32 * t + 32, 7, 0:P], cst[:, C_ONE:C_ONE + 32],
                                  work_c[:, k, P * t:P * t + P], start=(k == 0), stop=(k == KD - 1))
                last.then_inc(ss_mm, 1)

            def spread_rms(g, bank=1):
                pe.wait_ge(norm2_steps, N2 * g + N2)
                if bank == 1 and later(g):
                    pe.wait_ge(x3_steps, X3 * g - KD)
                for t in range(TT):
                    last = mm(banks[:, bank, P * t:P * t + P], row[:, t, :], nt2[:, 1, :], start=True, stop=True)
                last.then_inc(rb_mm, 1)

            def gate_hidden(f, c, alternate=False):
                base, back = (2 + 2 * (c % 2), 2) if alternate else (2, 1)
                if c == 0:
                    pe.wait_ge(x2s_hi, KD * f + 1)
                    if later(f) and not alternate:
                        pe.wait_ge(x3_tok, f)
                elif c >= back:
                    pe.wait_ge(h_steps, 2 * CH * f + 2 * (c - back) + 1)
                steps = [(part, n) for part in range(2) for n in range(6)]
                if c == 0:
                    steps.sort(key=lambda step: step[1] >= 4)
                for part, n in steps:
                    k, a, b = passes[n]
                    if c >= back and part and n == 0:
                        pe.wait_ge(h_steps, 2 * CH * f + 2 * (c - back) + 2)
                    if c == 0 and part == 0 and n == 1:
                        pe.wait_ge(x2s_hi, KD * f + KD)
                    if c == 0 and part == 0 and n >= 4:
                        pe.wait_ge(x2s_lo, KD * f + k + 1)
                    w = HID * part + P * c
                    last = mm(banks[:, base + part, :], gh[:, a, k, w:w + P], x2s[:, b, k, :],
                              start=(n == 0), stop=(n == 5))
                    if n == 5:
                        last.then_inc((gate_mm, hidden_mm)[part], 1)

            def ffn_out(f, c):
                pe.wait_ge(h_hi, CH * f + c + 1)
                for m, a, b in ((0, 0, 0), (0, 1, 0), (1, 0, 0), (1, 1, 0), (0, 0, 1), (1, 0, 1)):
                    if b and m == 0:
                        pe.wait_ge(h_lo, CH * f + c + 1)
                    last = mm(banks[:, m, :], wout[:, a, c, P * m:P * m + P], hs[:, c % 2, b, :],
                              start=(c == 0 and a == b == 0), stop=(c == CH - 1 and b == 1))
                last.then_inc(out_mm, 1)

            def transpose_out(f, base=2):
                for k in range(KD):
                    pe.wait_ge(x3_steps, X3 * f + KD + k + 1)
                    for t in range(TT):
                        c = 256 * (t % 2) + P * k
                        last = nc.tensor.transpose(banks[:, base + t // 2, c:c + P],
                                                   work_d[:, k, P * t:P * t + P], ident)
                last.then_inc(ft_mm, 1)

            def head(g, norm2=True, ln=True):
                if ln:
                    square_sums(g - 1)
                k_proj(g)
                if not later(g):
                    q_proj(g)
                if ln:
                    ffn_out(g - 2, CH - 1)
                elif norm2:
                    square_sums(g - 1)
                v_proj(g)
                if norm2:
                    spread_rms(g - 1)
                if ln:
                    transpose_out(g - 2)
                if later(g):
                    q_proj(g)

            def main(g, fed=True, more=True):
                f = g - 1
                if fed:
                    gate_hidden(f, 0)
                scores_for_max(g, 0)
                scores_for_max(g, 1)
                if fed:
                    gate_hidden(f, 1)
                    ffn_out(f, 0)
                scores_for_max(g, 2)
                scores_for_max(g, 3)
                if fed:
                    gate_hidden(f, 2)
                pe.wait_ge(max_ready, 4 * g + 4)
                if fed:
                    ffn_out(f, 1)
                transpose_max(g)
                if fed:
                    gate_hidden(f, 3)
                    scores(g, 0)
                    ffn_out(f, 2)
                    gate_hidden(f, 4)
                    scores(g, 1)
                    ffn_out(f, 3)
                    attend(g, 0)
                    scores(g, 2)
                    gate_hidden(f, 5)
                    scores(g, 3)
                    ffn_out(f, 4)
                    attend(g, 1)
                    gate_hidden(f, 6)
                else:
                    for n in range(3):
                        scores(g, n, alternate=True)
                    attend(g, 0)
                    scores(g, 3, alternate=True)
                    attend(g, 1)
                if more:
                    transpose_x(g + 1)
                if fed:
                    ffn_out(f, 5)
                else:
                    warm_up(wqk[:, 0, 0], WARM_OUTPUT)
                o_proj(g)
                if fed:
                    gate_hidden(f, 7, alternate=not more)
                    if more:
                        ffn_out(f, 6)

            pe.wait_ge(zeroed, 1)
            zeros = vblk[:, 0:2].rearrange("p b j e d -> p (b j e d)")
            warm_up(zeros, WARM_LOADS)
            setup_tables(FIRST_TABLES)
            warm_up(zeros, WARM_TABLES)
            transpose_x(0)
            setup_tables(OTHER_TABLES)
            setup_shift()
            warm_up(zeros, WARM_WEIGHTS)
            pe.wait_ge(stage_lo, 1)
            pe.wait_ge(stage_hi, 2)
            head(0, norm2=False, ln=False)
            pe.wait_ge(identb_ready, 2)
            main(0, fed=False)
            pe.wait_ge(selectors_ready, 2)
            head(1, ln=False)
            pe.wait_ge(stage_hi, len(chunks))
            pe.wait_ge(stage_lo, len(chunks))
            main(1)
            head(2)
            with pe.Fori(2, GROUPS - 1) as i:
                main(i)
                head(i + 1)
            main(GROUPS - 1, more=False)
            square_sums(GROUPS - 1)
            ffn_out(GROUPS - 2, CH - 2)
            ffn_out(GROUPS - 2, CH - 1)
            spread_rms(GROUPS - 1, 6)
            warm_up(wqk[:, 0, 0], WARM_NORM, 7)
            for c in range(2):
                gate_hidden(GROUPS - 1, c, alternate=True)
            transpose_out(GROUPS - 2, 6)
            for c in range(2, CH):
                gate_hidden(GROUPS - 1, c, alternate=True)
                ffn_out(GROUPS - 1, c - 2)
            for c in range(CH - 2, CH):
                ffn_out(GROUPS - 1, c)
            transpose_out(GROUPS - 1)

        @block.scalar
        def _(act):
            def cut_hi(n):
                act.wait_ge(ld_stage[n % 2], 16 * (n // 2 + 1))
                nc.scalar.activation(chunks[n][1], stage_view(n), ACT.Copy).then_inc(stage_hi, 1)

            def xs_split(g):
                act.wait_ge(xn_beta, g + 1)
                nc.scalar.activation(xs[:, 0], xn[:, :, :], ACT.Copy).then_inc(xs_hi, 1)

            def k_out(g):
                act.wait_ge(k_mm, g + 1)
                nc.scalar.activation(kTb[:, :, :], banks[:, 4:6, :], ACT.Copy).then_inc(k_ready, 1)
                for e in range(2):
                    nc.scalar.activation(kpar[:, :, :, e, :], by_seq(banks[:, 4:6, :]), ACT.Copy,
                                         scale=cst[:, C_PAR + e:C_PAR + e + 1]).then_inc(k_ready, 1)

            def keep_v(g):
                act.wait_ge(v_mm, g + 1)
                nc.scalar.activation(v_kept, banks[:, 6:8, :].rearrange("p k n -> p (k n)"), ACT.Copy)\
                    .then_inc(v_out, 1)

            def place_v(g, src, same):
                by_tile = vblk[:, :, :, :, :].rearrange("p (t s) j e d -> p t s j e d", s=2)
                v = src.rearrange("p (t j e d) -> p t j e d", t=TT, e=2, d=DH)
                for e in range(2):
                    r = slice(64 * e, 64 * e + 64)
                    nc.scalar.activation(by_tile[r, :, e if same else 1 - e, :, e, :], v[r, :, :, e, :], ACT.Copy)\
                        .then_inc(v_ready, 1)

            def place_v_kept(g):
                act.wait_ge(v_out, g + 1)
                place_v(g, v_kept, True)

            def place_v_swapped(g):
                act.wait_ge(v_moved, 32 * g + 32)
                place_v(g, v_swapped, False)

            def tanh(f, c, base=2):
                act.wait_ge(gate_mm, CH * f + c + 1)
                if c == 0 and later(f):
                    act.wait_ge(x3_steps, X3 * f)
                if c >= 2 or later(f):
                    act.wait_ge(h_lo, CH * f + c - 1)
                nc.scalar.activation(act_t[:, c % 2, :], banks[:, base, :], ACT.Tanh, scale=0.5)\
                    .then_inc(tanh_ready, 1)

            def hidden_hi(f, c):
                act.wait_ge(h_steps, 2 * CH * f + 2 * c + 2)
                if c >= 2 or later(f):
                    act.wait_ge(out_mm, CH * f + c - 1)
                nc.scalar.activation(hs[:, c % 2, 0, :], act_t[:, c % 2, :], ACT.Copy).then_inc(h_hi, 1)

            def exp(g, n, base=4):
                act.wait_ge(st_mm, 4 * g + n + 1)
                if n >= 2 or later(g):
                    act.wait_ge(o_mm, 2 * g + n // 2)
                b = 4 * (n % 2)
                nc.scalar.activation(pt[:, b:b + 4].rearrange("p b j q -> p (b j q)"),
                                     banks[:, base:base + 2, :].rearrange("p k n -> p (k n)"), ACT.Exp,
                                     scale=SCALE).then_inc(p_ready, 1)

            def o_split(g, h):
                act.wait_ge(o_steps, 4 * g + 2 * h + 2)
                nc.scalar.activation(os_[:, 0, h, :], work_c[:, 1, :], ACT.Copy).then_inc(o_hi, 1)

            def square(g):
                act.wait_ge(x2_steps, 2 * g + 2)
                act.wait_ge(o_lo, 2 * g + 2)
                nc.scalar.activation(work_c[:, :, :], x2[:, :, :], ACT.Square).then_inc(sq_ready, 1)

            def x2_split(g):
                for k in range(KD):
                    act.wait_ge(x2n_steps, 2 * KD * g + KD + k + 1)
                    nc.scalar.activation(x2s[:, 0, k], work_b[:, k, :], ACT.Copy).then_inc(x2s_hi, 1)

            def copy_x3(f, base=2):
                act.wait_ge(ft_mm, f + 1)
                if later(f):
                    act.wait_ge(out_stored, 16 * f)
                nc.scalar.activation(final[:, :, :].rearrange("p t n -> p (t n)"),
                                     banks[:, base:base + 2, :].rearrange("p k n -> p (k n)"), ACT.Copy)\
                    .then_inc(x3_tok, 1)

            def keep_x2(f):
                if later(f):
                    act.wait_ge(ft_mm, f)
                nc.scalar.activation(work_d[:, :, :], x2[:, :, :], ACT.Copy).then_inc(x2_kept, 1)

            def feed(f, c, base=2):
                tanh(f, c, base)
                hidden_hi(f, c)

            def head(g, norm2=True, ln=True):
                k_out(g)
                keep_v(g)
                place_v_kept(g)
                if not later(g):
                    for n in range(EARLY, EARLY + 2):
                        cut_hi(n)
                if ln:
                    copy_x3(g - 2)
                if norm2:
                    x2_split(g - 1)
                place_v_swapped(g)

            def main(g, fed=True, more=True):
                f = g - 1

                def fill(c):
                    if fed:
                        feed(f, c)
                    else:
                        for n in cut_in_slot(c):
                            cut_hi(n)
                for c in range(4 if fed else 3):
                    fill(c)
                    if fed and c == 0:
                        keep_x2(f)
                odd = 4 if fed else 2
                exp(g, 0)
                fill(4 if fed else 3)
                exp(g, 1, odd)
                if not fed:
                    fill(4)
                exp(g, 2)
                if not fed:
                    exp(g, 3, odd)
                o_split(g, 0)
                fill(5)
                if fed:
                    exp(g, 3, odd)
                o_split(g, 1)
                fill(6)
                if more:
                    xs_split(g + 1)
                if fed:
                    tanh(f, 7, 2 if more else 4)
                square(g)
                if fed:
                    hidden_hi(f, 7)

            cut_hi(0)
            cut_hi(1)
            xs_split(0)
            cut_hi(2)
            act.wait_ge(zeroed, 1)
            head(0, norm2=False, ln=False)
            act.wait_ge(setup_dve, SETUP_TANH)
            nc.scalar.activation(cvec[0:B], cvec[0:B], ACT.Tanh).then_inc(setup_act, 1)
            main(0, fed=False)
            head(1, ln=False)
            act.wait_ge(shift_stored, 16)
            main(1)
            head(2)
            with act.Fori(2, GROUPS - 1) as i:
                main(i)
                head(i + 1)
            main(GROUPS - 1, more=False)
            x2_split(GROUPS - 1)
            for c in range(CH):
                feed(GROUPS - 1, c, 2 + 2 * (c % 2))
                if c == 1:
                    copy_x3(GROUPS - 2, 6)
                    keep_x2(GROUPS - 1)

        @block.vector
        def _(dve):
            V = nc.vector

            def rsqrt(steps, n, v, y, t):
                V.tensor_scalar(y.bitcast(I32), v.bitcast(I32), -0.5, RSQRT_MAGIC, ALU.mult, ALU.add)\
                    .then_inc(steps, 1)
                dve.wait_ge(steps, n + 1)
                for r in range(NEWTON):
                    V.tensor_tensor(t, y, y, ALU.mult).then_inc(steps, 1)
                    dve.wait_ge(steps, n + 3 * r + 2)
                    V.scalar_tensor_tensor(out=t, in0=t, scalar=-0.5, in1=v, op0=ALU.mult, op1=ALU.mult)\
                        .then_inc(steps, 1)
                    dve.wait_ge(steps, n + 3 * r + 3)
                    V.scalar_tensor_tensor(out=y, in0=t, scalar=1.5, in1=y, op0=ALU.add, op1=ALU.mult)\
                        .then_inc(steps, 1)
                    dve.wait_ge(steps, n + 3 * r + 4)

            def setup_identity():
                dve.wait_ge(ld_tables, LD_TABLE)
                for e in range(2):
                    V.tensor_copy(identb[64 * e:64 * e + 64, :], ident[64 * e:64 * e + 64, 64 * e:64 * e + 64])\
                        .then_inc(identb_ready, 1)

            def setup_tables(names, n):
                dve.wait_ge(tables_mm, n)
                V.tensor_copy(tabs[:, names[0]:names[-1] + 1].rearrange("p t k b -> p (t k b)"),
                              banks[:, TABLE_BANK[names], 0:len(names) * KD * B]).then_inc(tables_ready, 1)

            def setup_shift():
                dve.wait_ge(ld_lin, LD_SHIFT)
                dve.wait_ge(shift_mm, 1)
                V.tensor_tensor(cvec[0:B], banks[0:B, 2, 0:D], linb_b[0:B], ALU.add).then_inc(setup_dve, 1)
                V.tensor_tensor(w2[:, :], lnw_b, lnw_b, ALU.mult).then_inc(setup_dve, 1)

            def finish_shift():
                dve.wait_ge(setup_act, 1)
                V.tensor_tensor(cvec[0:B], cvec[0:B], lnb_b[0:B], ALU.add).then_inc(setup_dve, 1)
                dve.wait_ge(setup_dve, 3)
                V.tensor_tensor(cvec[0:B], cvec[0:B], lnw_b[0:B], ALU.mult).then_inc(setup_dve, 1)
                dve.wait_ge(setup_dve, 4)
                V.tensor_tensor(cvec[0:B], cvec[0:B], lnb_b[0:B], ALU.add).then_inc(setup_dve, 1)

            def cut_lo(n):
                dve.wait_ge(stage_hi, n + 1)
                V.tensor_tensor(chunks[n][2], stage_view(n), chunks[n][1].bitcast(F32), ALU.subtract)\
                    .then_inc(stage_lo, 1)

            def stats_x(g):
                dve.wait_ge(ld_x, 16 * g + 16)
                for t in range(TT):
                    V.bn_stats(stat[:, 0, t, :], xtok[:, t, :]).then_inc(x_stats, 1)
                dve.wait_ge(x_stats, XS * g + TT)
                V.memset(nt1[:, 2, 0, :], 0.0)
                for t in range(TT):
                    V.bn_aggr(mv[:, 0, t, :], stat[:, 0, t, :]).then_inc(x_stats, 1)
                dve.wait_ge(x_stats, XS * g + 2 * TT)
                V.tensor_tensor(nt1[:, 2, 0, :], mv[:, 0, :, 0], mv[:, 0, :, 0], ALU.mult).then_inc(x_stats, 1)
                dve.wait_ge(x_stats, XS * g + 2 * TT + 1)
                V.scalar_tensor_tensor(out=nt1[:, 0, 0, :], in0=nt1[:, 2, 0, :], scalar=EPS_RMS,
                                       in1=mv[:, 0, :, 1], op0=ALU.add, op1=ALU.add).then_inc(x_stats, 1)

            def stats_x3(f, tile=lambda t: final[:, t, :]):
                for t in range(TT):
                    V.bn_stats(stat[:, 1, t, :], tile(t)).then_inc(ln_stats, 1)
                dve.wait_ge(ln_stats, LS * f + TT)
                V.memset(nt1[:, 2, 1, :], 0.0)
                for t in range(TT):
                    V.bn_aggr(mv[:, 1, t, :], stat[:, 1, t, :]).then_inc(ln_stats, 1)
                dve.wait_ge(ln_stats, LS * f + 2 * TT)
                V.tensor_scalar(nt1[:, 0, 1, :], mv[:, 1, :, 1], EPS_LN, None, ALU.add).then_inc(ln_stats, 1)

            def rsqrt_both(n):
                v, y, t = (nt1[:, i].rearrange("p a t -> p (a t)") for i in range(3))
                rsqrt(norm1_steps, RS * n, v, y, t)

            def scale_xn(g):
                dve.wait_ge(xt_mm, g + 1)
                V.tensor_tensor(by_seq(xn[:, :, :]), by_seq(banks[:, 4:6, :]), table(GA, g), ALU.mult)\
                    .then_inc(xn_gamma, 1)

            def shift_xn(g):
                dve.wait_ge(xn_gamma, g + 1)
                V.tensor_tensor(by_seq(xn[:, :, :]), by_seq(xn[:, :, :]), table(BA, g), ALU.add).then_inc(xn_beta, 1)

            def xs_split(g):
                dve.wait_ge(xs_hi, g + 1)
                V.tensor_tensor(xs[:, 1], xn[:, :, :], xs[:, 0].bitcast(F32), ALU.subtract).then_inc(xs_lo, 1)

            def q_out(g):
                base = 4 if later(g) else 0
                dve.wait_ge(q_mm, g + 1)
                for h in range(G):
                    V.tensor_copy(qT[:, h, :], banks[:, base + h, :]).then_inc(q_ready, 1)
                for h in range(G):
                    dve.wait_ge(q_ready, 6 * g + h + 1)
                    for e in range(2):
                        V.tensor_scalar(qpar[:, h, :, e, :], by_token(qT[:, h, :]),
                                        cst[:, C_PAR + e:C_PAR + e + 1], None, ALU.mult).then_inc(q_ready, 1)

            def max_over_keys(g, n):
                dve.wait_ge(s_mm, 4 * g + n + 1)
                base = bank_of_s(g, n)
                V.tensor_reduce(smax[:, 16 * n:16 * n + 16],
                                banks[:, base:base + 2, :].rearrange("p k (r c) -> p (k r) c", c=L),
                                AX.X, ALU.max).then_inc(max_ready, 1)

            def negate_max(g):
                dve.wait_ge(mt_mm, g + 1)
                V.tensor_tensor(negmax[:, :, :], max_t.unsqueeze(1).to_broadcast([P, J, L]),
                                cst[:, C_NEG:C_NEG + J].unsqueeze(2).to_broadcast([P, J, L]), ALU.mult)\
                    .then_inc(negmax_ready, 1)

            def normalise(g, h):
                dve.wait_ge(den_mm, 2 * g + h + 1)
                if h == 0:
                    dve.wait_ge(v_ready, 4 * g + 4)
                V.reciprocal(work_c[:, 0, :], banks[:, 7, :]).then_inc(o_steps, 1)
                dve.wait_ge(o_steps, 4 * g + 2 * h + 1)
                dve.wait_ge(o_mm, 2 * g + h + 1)
                if h:
                    dve.wait_ge(o_hi, 2 * g + 1)
                    dve.wait_ge(o_lo, 2 * g + 1)
                V.tensor_tensor(work_c[:, 1, :], banks[:, 6, :], work_c[:, 0, :], ALU.mult).then_inc(o_steps, 1)

            def residual1(g):
                dve.wait_ge(op_mm, g + 1)
                dve.wait_ge(ld_res, 16 * g + 16)
                V.tensor_tensor(by_seq(work_b[:, :, :]), by_seq(banks[:, 6:8, :]), table(AA, g), ALU.mult)\
                    .then_inc(x2_steps, 1)
                dve.wait_ge(x2_steps, 2 * g + 1)
                V.tensor_tensor(x2[:, :, :], work_b[:, :, :], xres[:, :, :], ALU.add).then_inc(x2_steps, 1)

            def norm2(g):
                v, y, t = (nt2[:, i, :] for i in range(3))
                dve.wait_ge(ss_mm, g + 1)
                V.tensor_scalar(v, banks[:, 7, 0:P], 1.0 / D, EPS_RMS, ALU.mult, ALU.add).then_inc(norm2_steps, 1)
                dve.wait_ge(norm2_steps, N2 * g + 1)
                rsqrt(norm2_steps, N2 * g + 1, v, y, t)

            def scale_x2(g, bank=1):
                dve.wait_ge(x2_gamma, g + 1)
                dve.wait_ge(rb_mm, g + 1)
                for k in range(KD):
                    V.tensor_tensor(work_b[:, k, :], work_b[:, k, :], banks[:, bank, :], ALU.mult)\
                        .then_inc(x2n_steps, 1)
                for k in range(KD):
                    dve.wait_ge(x2n_steps, 2 * KD * g + k + 1)
                    V.tensor_tensor(by_token(work_b[:, k, :]), by_token(work_b[:, k, :]), table(BF, g, k), ALU.add)\
                        .then_inc(x2n_steps, 1)

            def feed(f, c, base=2):
                a = act_t[:, c % 2, :]
                dve.wait_ge(tanh_ready, CH * f + c + 1)
                V.scalar_tensor_tensor(out=a, in0=a, scalar=1.0, in1=banks[:, base, :], op0=ALU.add,
                                       op1=ALU.mult).then_inc(h_steps, 1)
                dve.wait_ge(h_steps, 2 * CH * f + 2 * c + 1)
                dve.wait_ge(hidden_mm, CH * f + c + 1)
                V.scalar_tensor_tensor(out=a, in0=a, scalar=0.5, in1=banks[:, base + 1, :], op0=ALU.mult,
                                       op1=ALU.mult).then_inc(h_steps, 1)

            def residual2(f):
                dve.wait_ge(out_mm, CH * f + CH)
                dve.wait_ge(h_lo, CH * f + CH)
                for m in range(KD):
                    V.scalar_tensor_tensor(
                        out=by_token(act_t[:, m, :]), in0=by_token(banks[:, m, :]), scalar=outb[:, m:m + 1],
                        in1=table(AF, f, m), op0=ALU.add, op1=ALU.mult).then_inc(x3_steps, 1)
                dve.wait_ge(x2_kept, f + 1)
                for m in range(KD):
                    dve.wait_ge(x3_steps, X3 * f + m + 1)
                    V.tensor_tensor(work_d[:, m, :], work_d[:, m, :], act_t[:, m, :], ALU.add).then_inc(x3_steps, 1)

            def finish(f, tile=lambda t: final[:, t, :]):
                for t in range(TT):
                    V.scalar_tensor_tensor(out=final[:, t, :], in0=tile(t), scalar=mv[:, 1, t, 0:1],
                                           in1=w2[:, :], op0=ALU.subtract, op1=ALU.mult).then_inc(final_steps, 1)
                dve.wait_ge(ld_shift, 32 * f + 32)
                for t in range(TT):
                    dve.wait_ge(final_steps, FS * f + t + 1)
                    V.scalar_tensor_tensor(out=final[:, t, :], in0=final[:, t, :], scalar=nt1[:, 1, 1, t:t + 1],
                                           in1=shift[:, t, :], op0=ALU.mult, op1=ALU.add).then_inc(final_steps, 1)

            def head(g, norm2_=True, ln=True):
                if norm2_:
                    norm2(g - 1)
                if ln:
                    residual2(g - 2)
                if norm2_:
                    scale_x2(g - 1)
                q_out(g)

            def main(g, fed=True, more=True, ln=True):
                f = g - 1

                def fill(c):
                    if fed:
                        feed(f, c)
                    else:
                        for n in cut_in_slot(c):
                            cut_lo(n)
                fill(0)
                max_over_keys(g, 0)
                max_over_keys(g, 1)
                fill(1)
                max_over_keys(g, 2)
                max_over_keys(g, 3)
                fill(2)
                negate_max(g)
                if not fed:
                    for n in range(EARLY, EARLY + 2):
                        cut_lo(n)
                    finish_shift()
                if more:
                    stats_x(g + 1)
                fill(3)
                if ln:
                    dve.wait_ge(x3_tok, g - 1)
                    stats_x3(g - 2)
                if more:
                    dve.wait_ge(x_stats, XS * (g + 2))
                if ln:
                    dve.wait_ge(ln_stats, LS * (g - 1))
                rsqrt_both(g + 1)
                if fed:
                    fill(4)
                if ln:
                    finish(g - 2)
                normalise(g, 0)
                if not fed:
                    fill(4)
                fill(5)
                normalise(g, 1)
                fill(6)
                if more:
                    scale_xn(g + 1)
                if not fed:
                    shift_xn(g + 1)
                    xs_split(g + 1)
                residual1(g)
                if fed:
                    feed(f, 7, 2 if more else 4)

            V.memset(nt1[:, :, :, :], 1.0).then_inc(nt1_set, 1)
            dve.wait_ge(nt1_set, 1)
            stats_x(0)
            dve.wait_ge(x_stats, XS)
            rsqrt_both(0)
            for h in range(2):
                tiles = slice(TT // 2 * h, TT // 2 * h + TT // 2)
                V.tensor_tensor(xtok[:, tiles, :], xtok[:, tiles, :],
                                nt1[:, 1, 0, tiles].unsqueeze(2).to_broadcast([P, TT // 2, D]), ALU.mult)\
                    .then_inc(xs_scaled, 1)
            setup_tables(FIRST_TABLES, 1)
            dve.wait_ge(tables_ready, 1)
            scale_xn(0)
            shift_xn(0)
            cut_lo(0)
            xs_split(0)
            cut_lo(1)
            setup_tables(OTHER_TABLES, 2)
            cut_lo(2)
            setup_identity()
            setup_shift()
            head(0, norm2_=False, ln=False)
            main(0, fed=False, ln=False)
            head(1, ln=False)
            main(1, ln=False)
            head(2)
            with dve.Fori(2, GROUPS - 1) as i:
                main(i)
                head(i + 1)
            main(GROUPS - 1, more=False)
            norm2(GROUPS - 1)
            scale_x2(GROUPS - 1, 6)
            residual2(GROUPS - 2)
            for c in range(CH):
                feed(GROUPS - 1, c, 2 + 2 * (c % 2))
                if c == 2:
                    dve.wait_ge(x3_tok, GROUPS - 1)
                    stats_x3(GROUPS - 2)
                    dve.wait_ge(ln_stats, LS * (GROUPS - 1))
                    rsqrt_both(GROUPS + 1)
                if c == 4:
                    finish(GROUPS - 2)
            residual2(GROUPS - 1)

            def in_banks(t):
                return banks[:, 2 + t // 2, 256 * (t % 2):256 * (t % 2) + D]

            dve.wait_ge(ft_mm, GROUPS)
            stats_x3(GROUPS - 1, in_banks)
            dve.wait_ge(ln_stats, LS * GROUPS)
            rsqrt_both(GROUPS + 2)
            dve.wait_ge(out_stored, 16 * (GROUPS - 1))
            finish(GROUPS - 1, in_banks)

        @block.gpsimd
        def _(pool):
            tt = nc.gpsimd.tensor_tensor

            def scale_x(g):
                pool.wait_ge(norm1_steps, RS * g + RS)
                tt(xtok[:, :, :], xtok[:, :, :], nt1[:, 1, 0, :].unsqueeze(2).to_broadcast([P, TT, D]),
                   ALU.mult).then_inc(xs_scaled, 1)

            def shift_xn(g):
                pool.wait_ge(xn_gamma, g + 1)
                tt(by_seq(xn[:, :, :]), by_seq(xn[:, :, :]), table(BA, g), ALU.add).then_inc(xn_beta, 1)

            def xs_split(g):
                pool.wait_ge(xs_hi, g + 1)
                tt(xs[:, 1], xn[:, :, :], xs[:, 0].bitcast(F32), ALU.subtract).then_inc(xs_lo, 1)

            def o_split(g, h):
                pool.wait_ge(o_hi, 2 * g + h + 1)
                tt(os_[:, 1, h, :], work_c[:, 1, :], os_[:, 0, h, :].bitcast(F32), ALU.subtract).then_inc(o_lo, 1)

            def x2_by_gamma(g):
                pool.wait_ge(x2_steps, 2 * g + 2)
                tt(by_seq(work_b[:, :, :]), by_seq(x2[:, :, :]), table(GF, g), ALU.mult).then_inc(x2_gamma, 1)

            def x2_split(g):
                for k in range(KD):
                    pool.wait_ge(x2s_hi, KD * g + k + 1)
                    tt(x2s[:, 1, k], work_b[:, k, :], x2s[:, 0, k].bitcast(F32), ALU.subtract).then_inc(x2s_lo, 1)

            def hidden_lo(f, c):
                pool.wait_ge(h_hi, CH * f + c + 1)
                tt(hs[:, c % 2, 1, :], act_t[:, c % 2, :], hs[:, c % 2, 0, :].bitcast(F32), ALU.subtract)\
                    .then_inc(h_lo, 1)

            def main(g, fed=True, more=True):
                f = g - 1

                def fill(c):
                    if fed:
                        hidden_lo(f, c)
                if not later(g):
                    pool.wait_ge(tables_ready, 2)
                for c in range(5):
                    fill(c)
                    if more and c == 3:
                        scale_x(g + 1)
                o_split(g, 0)
                fill(5)
                o_split(g, 1)
                if fed and more:
                    shift_xn(g + 1)
                fill(6)
                if fed and more:
                    xs_split(g + 1)
                fill(7)
                x2_by_gamma(g)

            nc.gpsimd.memset(vblk[:, :, :, :, :], 0.0).then_inc(zeroed, 1)
            nc.gpsimd.memset(kpair[:, :, :, :], 0.0).then_inc(zeroed, 1)
            nc.gpsimd.memset(qpair[:, :, :, :], 0.0).then_inc(zeroed, 1)
            pool.wait_ge(ld_tables, LD_TABLE)
            nc.gpsimd.tensor_copy(sel[:, :, :].rearrange("p c (e k) -> p (c e) k", e=2),
                                  cst[:, C_SEL:C_SEL + 2 * G * SEQ].unsqueeze(2).to_broadcast([P, 2 * G * SEQ, L]))\
                .then_inc(selectors_ready, 1)
            nc.gpsimd.tensor_copy(row[:, :, :], cst[:, C_ROW:C_ROW + TT].unsqueeze(2).to_broadcast([P, TT, P]))\
                .then_inc(selectors_ready, 1)
            main(0, fed=False)
            x2_split(0)
            main(1)
            x2_split(1)
            with pool.Fori(2, GROUPS - 1) as i:
                main(i)
                x2_split(i)
            main(GROUPS - 1, more=False)
            x2_split(GROUPS - 1)
            for c in range(CH):
                hidden_lo(GROUPS - 1, c)


def kernel(x, cond_256, L1_cond_weight, L1_cond_bias, L1_cond_lin_w, L1_cond_lin_b, **w):
    import concourse.bacc as bacc
    from concourse.bass_utils import run_bass_kernel_spmd

    def layer0(name):
        return np.asarray(w["L0_cond_" + name])

    x = np.asarray(x)
    arrays = dict(
        x=x,
        xT=x.reshape(B * L, D).T,
        condT=np.asarray(cond_256).T,
        tabT=np.stack([layer0(t + "_w").T for t in TABLES], axis=1),
        linT=np.asarray(L1_cond_lin_w).T,
        linb=np.asarray(L1_cond_lin_b).reshape(1, D),
        lnw=np.asarray(L1_cond_weight).reshape(1, D),
        lnb=np.asarray(L1_cond_bias).reshape(1, D),
        wqkT=np.concatenate([layer0("W_q").T, layer0("W_k").T], axis=1),
        wvT=layer0("W_v").T,
        woT=layer0("W_o").T,
        ghT=np.concatenate([layer0("gate_w").T, layer0("hidden_w").T], axis=1),
        outT=layer0("out_w").T,
        outb=layer0("out_b").reshape(KD, P).T,
        consts=shape_constants(),
    )
    arrays = {k + "_in": np.ascontiguousarray(a) for k, a in arrays.items()}
    nc = bacc.Bacc("TRN2", target_bir_lowering=False, num_devices=1)
    args = [nc.dram_tensor(k, a.shape, mybir.dt.from_np(a.dtype), kind="ExternalInput").ap()
            for k, a in arrays.items()]
    args.append(nc.dram_tensor("y", (B, L, D), F32, kind="ExternalOutput").ap())
    build(nc, *args)
    r = run_bass_kernel_spmd(nc, [arrays], core_ids=[0])
    return r.results[0]["y"]
```
